# Optimizing a Trainium2 kernel written in Bass

```python
import numpy as np
import jax
import jax.numpy as jnp

def _softmax(x, axis=-1):
    return jax.nn.softmax(x, axis=axis)

def _gelu(x):
    return jax.nn.gelu(x, approximate=True)

def _silu(x):
    return jax.nn.silu(x)

def _sigmoid(x):
    return jax.nn.sigmoid(x)

def _layernorm(x, axis=-1, eps=1e-05):
    m = jnp.mean(x, axis=axis, keepdims=True)
    v = jnp.var(x, axis=axis, keepdims=True)
    return (x - m) / jnp.sqrt(v + eps)

def _scatter_add(tgt, idx, src, axis=0):
    return tgt.at[idx].add(src)

def _segment_sum(src, seg, n):
    return jax.ops.segment_sum(src, seg, n)
kernel_name = 'mk_decoder_postln_d1_seqx_r4_c05083'

def setup_inputs(seed: int=0):
    np.random.seed(seed)
    _w = jnp.asarray

    def _rec_inputs():
        import jax
        import jax.numpy as jnp
        _rk = jax.random.key(seed)
        x = -0.0002928 + 1 * jax.random.normal(jax.random.fold_in(_rk, 1), (16, 100, 256), jnp.float32)
        _lenS = 100 - jax.random.randint(jax.random.fold_in(_rk, 7), (16,), 0, max(1, 100 // 4) + 1, jnp.int32)
        _lenS2 = 361 - jax.random.randint(jax.random.fold_in(_rk, 8), (16,), 0, max(1, 361 // 4) + 1, jnp.int32)
        _ctx_1024P = jax.random.normal(jax.random.fold_in(_rk, 11), (16, 16, 256), jnp.float32)
        _ctx_1024c = jax.random.dirichlet(jax.random.fold_in(_rk, 511), 0.3 * jnp.ones((16,), jnp.float32), (16, 361))
        _ctx_1024t = jnp.einsum('bsk,bkd->bsd', _ctx_1024c, _ctx_1024P)
        _ctx_1024t = _ctx_1024t * jax.lax.rsqrt(jnp.mean(jnp.square(_ctx_1024t)) + 1e-12) * 0.953939
        ctx_1024 = -1.39393e-06 + 0.999914 * (_ctx_1024t + 0.3 * jax.random.normal(jax.random.fold_in(_rk, 611), (16, 361, 256), jnp.float32))
        return (x, ctx_1024)
    x, ctx_1024 = _rec_inputs()

    def _L0_attn_setup():
        import jax, jax.numpy as jnp
        import numpy as np
        B, L, D = (8, 512, 256)
        LEARNED = 64
        WINDOWS = (32.0, 64.0, 128.0, 256.0)

        def _forward(x, Wq, Wk, Wv, Wqkv, bqkv, Wop, W2, b2):
            dt = x.dtype
            Bs, Ls, Ds = x.shape
            windows = jnp.asarray(WINDOWS, dt)
            G = windows.shape[0]
            dh = Ds // G
            BIG = jnp.asarray(1e+18, dt)
            q_in = x @ Wq.T
            _k_unused = x @ Wk.T
            _v_unused = x @ Wv.T
            qkv = (q_in @ Wqkv.T + bqkv).reshape(Bs, Ls, 3, Ds)
            q = qkv[:, :, 0].reshape(Bs, Ls, G, dh)
            k = qkv[:, :, 1].reshape(Bs, Ls, G, dh)
            v = qkv[:, :, 2].reshape(Bs, Ls, G, dh)
            scale = jnp.asarray(1.0 / np.sqrt(Ls), dt)
            scores = jnp.einsum('blgd,bmgd->bglm', q, k) * scale
            h = jax.nn.relu(q_in) @ Wop.T
            dx = jax.nn.sigmoid(h @ W2.T + b2) * Ls
            dx_g = dx[:, None, :, :] + windows[None, :, None, None]
            idx = jnp.arange(Ls)
            dist = jnp.abs(idx[:, None] - idx[None, :]).astype(dt)
            win_mask = jnp.where(idx[None, :] < idx[:, None], BIG, dist)
            masked = jnp.where(win_mask[None, None] > dx_g, -BIG, scores)
            s2 = masked + scores
            attn = jax.nn.softmax(s2, axis=-1)
            out = jnp.einsum('bglm,bmgd->blgd', attn, v).reshape(Bs, Ls, Ds)
            return out
        key = jax.random.key(seed)
        ks = jax.random.split(key, 9)
        s = 0.02
        return {'x': jax.random.normal(ks[0], (B, L, D), jnp.float32), 'Wq': jax.random.normal(ks[1], (D, D), jnp.float32) * s, 'Wk': jax.random.normal(ks[2], (D, D), jnp.float32) * s, 'Wv': jax.random.normal(ks[3], (D, D), jnp.float32) * s, 'Wqkv': jax.random.normal(ks[4], (3 * D, D), jnp.float32) * s, 'bqkv': jnp.zeros((3 * D,), jnp.float32), 'Wop': jax.random.normal(ks[5], (LEARNED, D), jnp.float32) * s, 'W2': jax.random.normal(ks[6], (1, LEARNED), jnp.float32) * s, 'b2': jnp.zeros((1,), jnp.float32)}
    _L0_attn_all = _L0_attn_setup()
    _L0_attn_in = {k: v for k, v in _L0_attn_all.items() if k in ('Wq', 'Wk', 'Wv', 'Wqkv', 'bqkv', 'Wop', 'W2', 'b2')}
    del _L0_attn_all

    def _L0_xattn_setup():
        import jax, jax.numpy as jnp
        import numpy as np
        DIM = 256
        NUM_HEAD = 16
        DIM_HEAD = DIM // NUM_HEAD
        key = jax.random.key(seed)
        ks = jax.random.split(key, 11)
        B, S = (2, 512)
        s = 1.0 / np.sqrt(DIM)
        return {'query': jax.random.normal(ks[0], (B, S, DIM), jnp.float32), 'key': jax.random.normal(ks[1], (B, S, DIM), jnp.float32), 'value': jax.random.normal(ks[2], (B, S, DIM), jnp.float32), 'wq': jax.random.normal(ks[3], (DIM, DIM), jnp.float32) * s, 'bq': jax.random.normal(ks[4], (DIM,), jnp.float32) * s, 'wk': jax.random.normal(ks[5], (DIM, DIM), jnp.float32) * s, 'bk': jax.random.normal(ks[6], (DIM,), jnp.float32) * s, 'wv': jax.random.normal(ks[7], (DIM, DIM), jnp.float32) * s, 'bv': jax.random.normal(ks[8], (DIM,), jnp.float32) * s, 'wo': jax.random.normal(ks[9], (DIM, DIM), jnp.float32) * s, 'bo': jax.random.normal(ks[10], (DIM,), jnp.float32) * s}
    _L0_xattn_all = _L0_xattn_setup()
    _L0_xattn_in = {k: v for k, v in _L0_xattn_all.items() if k in ('wq', 'bq', 'wk', 'bk', 'wv', 'bv', 'wo', 'bo')}
    del _L0_xattn_all

    def _L0_ffn_setup():
        import jax, jax.numpy as jnp
        import numpy as np
        D, F, E, K = (256, 688, 8, 2)
        key = jax.random.key(seed)
        k0, k1, k2, k3, k4 = jax.random.split(key, 5)
        s = 0.02
        x = jax.random.normal(k0, (2, 128, D), jnp.float32)
        Ws = jax.random.normal(k1, (D, E), jnp.float32) * s
        bs = jnp.zeros((E,), jnp.float32)
        Wg = jax.random.normal(k2, (E, D, F), jnp.float32) * s
        Wu = jax.random.normal(k3, (E, D, F), jnp.float32) * s
        Wd = jax.random.normal(k4, (E, F, D), jnp.float32) * s
        return {'x': x, 'Ws': Ws, 'bs': bs, 'Wg': Wg, 'Wu': Wu, 'Wd': Wd}
    _L0_ffn_all = _L0_ffn_setup()
    _L0_ffn_in = {k: v for k, v in _L0_ffn_all.items() if k in ('Ws', 'bs', 'Wg', 'Wu', 'Wd')}
    del _L0_ffn_all
    return {'x': x, 'ctx_1024': ctx_1024, 'L0_attn_Wq': _L0_attn_in['Wq'], 'L0_attn_Wk': _L0_attn_in['Wk'], 'L0_attn_Wv': _L0_attn_in['Wv'], 'L0_attn_Wqkv': _L0_attn_in['Wqkv'], 'L0_attn_bqkv': _L0_attn_in['bqkv'], 'L0_attn_Wop': _L0_attn_in['Wop'], 'L0_attn_W2': _L0_attn_in['W2'], 'L0_attn_b2': _L0_attn_in['b2'], 'L0_xattn_wq': _L0_xattn_in['wq'], 'L0_xattn_bq': _L0_xattn_in['bq'], 'L0_xattn_wk': _L0_xattn_in['wk'], 'L0_xattn_bk': _L0_xattn_in['bk'], 'L0_xattn_wv': _L0_xattn_in['wv'], 'L0_xattn_bv': _L0_xattn_in['bv'], 'L0_xattn_wo': _L0_xattn_in['wo'], 'L0_xattn_bo': _L0_xattn_in['bo'], 'L0_ffn_Ws': _L0_ffn_in['Ws'], 'L0_ffn_bs': _L0_ffn_in['bs'], 'L0_ffn_Wg': _L0_ffn_in['Wg'], 'L0_ffn_Wu': _L0_ffn_in['Wu'], 'L0_ffn_Wd': _L0_ffn_in['Wd']}

def reference(x, ctx_1024, L0_attn_Wq, L0_attn_Wk, L0_attn_Wv, L0_attn_Wqkv, L0_attn_bqkv, L0_attn_Wop, L0_attn_W2, L0_attn_b2, L0_xattn_wq, L0_xattn_bq, L0_xattn_wk, L0_xattn_bk, L0_xattn_wv, L0_xattn_bv, L0_xattn_wo, L0_xattn_bo, L0_ffn_Ws, L0_ffn_bs, L0_ffn_Wg, L0_ffn_Wu, L0_ffn_Wd):
    import jax
    import jax.numpy as jnp

    def _L0_attn_ref(x, Wq, Wk, Wv, Wqkv, bqkv, Wop, W2, b2):
        import jax, jax.numpy as jnp
        import numpy as np
        B, L, D = (8, 512, 256)
        LEARNED = 64
        WINDOWS = (32.0, 64.0, 128.0, 256.0)

        def _forward(x, Wq, Wk, Wv, Wqkv, bqkv, Wop, W2, b2):
            dt = x.dtype
            Bs, Ls, Ds = x.shape
            windows = jnp.asarray(WINDOWS, dt)
            G = windows.shape[0]
            dh = Ds // G
            BIG = jnp.asarray(1e+18, dt)
            q_in = x @ Wq.T
            _k_unused = x @ Wk.T
            _v_unused = x @ Wv.T
            qkv = (q_in @ Wqkv.T + bqkv).reshape(Bs, Ls, 3, Ds)
            q = qkv[:, :, 0].reshape(Bs, Ls, G, dh)
            k = qkv[:, :, 1].reshape(Bs, Ls, G, dh)
            v = qkv[:, :, 2].reshape(Bs, Ls, G, dh)
            scale = jnp.asarray(1.0 / np.sqrt(Ls), dt)
            scores = jnp.einsum('blgd,bmgd->bglm', q, k) * scale
            h = jax.nn.relu(q_in) @ Wop.T
            dx = jax.nn.sigmoid(h @ W2.T + b2) * Ls
            dx_g = dx[:, None, :, :] + windows[None, :, None, None]
            idx = jnp.arange(Ls)
            dist = jnp.abs(idx[:, None] - idx[None, :]).astype(dt)
            win_mask = jnp.where(idx[None, :] < idx[:, None], BIG, dist)
            masked = jnp.where(win_mask[None, None] > dx_g, -BIG, scores)
            s2 = masked + scores
            attn = jax.nn.softmax(s2, axis=-1)
            out = jnp.einsum('bglm,bmgd->blgd', attn, v).reshape(Bs, Ls, Ds)
            return out
        return _forward(x, Wq, Wk, Wv, Wqkv, bqkv, Wop, W2, b2)

    def _L0_xattn_ref(query, key, value, wq, bq, wk, bk, wv, bv, wo, bo):
        import jax, jax.numpy as jnp
        import numpy as np
        DIM = 256
        NUM_HEAD = 16
        DIM_HEAD = DIM // NUM_HEAD
        B, S, _ = query.shape

        def proj(x, w, b):
            y = x @ w.T + b
            return y.reshape(B, -1, NUM_HEAD, DIM_HEAD).transpose(0, 2, 1, 3)
        Q = proj(query, wq, bq).astype(jnp.float32)
        K = proj(key, wk, bk).astype(jnp.float32)
        V = proj(value, wv, bv).astype(jnp.float32)
        energy = jnp.einsum('bhqd,bhkd->bhqk', Q, K) / np.sqrt(DIM_HEAD).astype(np.float32)
        attn = jax.nn.softmax(energy, axis=-1)
        out = jnp.einsum('bhqk,bhkd->bhqd', attn, V)
        out = out.transpose(0, 2, 1, 3).reshape(B, S, DIM)
        return out @ wo.T + bo

    def _L0_ffn_ref(x, Ws, bs, Wg, Wu, Wd):
        import jax, jax.numpy as jnp
        import numpy as np
        D, F, E, K = (256, 688, 8, 2)
        b, n, d = x.shape
        xt = x.reshape(-1, d)
        logits = xt @ Ws + bs
        topk_w, topk_idx = jax.lax.top_k(logits, K)
        topk_w = jax.nn.softmax(topk_w, axis=-1)
        combine = jnp.sum(jax.nn.one_hot(topk_idx, E, dtype=xt.dtype) * topk_w[..., None], axis=1)
        g = jnp.einsum('td,edf->tef', xt, Wg)
        u = jnp.einsum('td,edf->tef', xt, Wu)
        h = jax.nn.silu(g) * u
        y = jnp.einsum('tef,efd->ted', h, Wd)
        out = jnp.einsum('ted,te->td', y, combine)
        return out.reshape(b, n, d)
    x = _layernorm(x + _L0_attn_ref(x, L0_attn_Wq, L0_attn_Wk, L0_attn_Wv, L0_attn_Wqkv, L0_attn_bqkv, L0_attn_Wop, L0_attn_W2, L0_attn_b2), axis=-1)
    x = _layernorm(x + _L0_xattn_ref(x, ctx_1024, ctx_1024, L0_xattn_wq, L0_xattn_bq, L0_xattn_wk, L0_xattn_bk, L0_xattn_wv, L0_xattn_bv, L0_xattn_wo, L0_xattn_bo), axis=-1)
    x = _layernorm(x + _L0_ffn_ref(x, L0_ffn_Ws, L0_ffn_bs, L0_ffn_Wg, L0_ffn_Wu, L0_ffn_Wd), axis=-1)
    return x

_drawn_inputs = setup_inputs


def setup_inputs(seed=0):
    import zlib

    import numpy as np

    out = dict(_drawn_inputs(seed))
    spreads = {'L0_attn_bqkv': (0.0, 0.1), 'L0_ffn_bs': (0.0, 0.799)}
    factors = {'L0_attn_Wop': 8.0,
     'L0_attn_W2': 8.0,
     'L0_xattn_bq': 4.609,
     'L0_xattn_bk': 8.0,
     'L0_ffn_Ws': 3.382,
     'L0_ffn_Wg': 2.913,
     'L0_ffn_Wu': 2.882,
     'L0_ffn_Wd': 2.877}
    for name, (base, spread) in spreads.items():
        noise = np.random.default_rng([zlib.crc32(name.encode()), seed]).standard_normal(out[name].shape)
        drawn = base * np.exp(spread * noise) if base else spread * noise
        out[name] = jnp.asarray(drawn.astype(out[name].dtype))
    for name, factor in factors.items():
        out[name] = (out[name] * factor).astype(out[name].dtype)
    return out
```

```python
from contextlib import ExitStack

import numpy as np

import concourse.bass as bass
from concourse import mybir

F32 = mybir.dt.float32
BF16 = mybir.dt.bfloat16
U32 = mybir.dt.uint32
I32 = mybir.dt.int32
ALU = mybir.AluOpType
ACT = mybir.ActivationFunctionType
AX_X = mybir.AxisListType.X

P = 128
NB, L, D = 16, 100, 256
T = NB * L
KC = D // P
EPS = 1e-5

G, DG = 4, 64
WINDOWS = (32.0, 64.0, 128.0, 256.0)
NW = sum(w < L - 1 for w in WINDOWS)
PAIRS = NB // 2
BIG = 1e18

CTX = 361
H, DH = 16, 16
NCH = 3
CH = (CTX - 1) // NCH
CM = CH + 1
KQ = CTX + L
SLOTS = 6
PARTS = 3
SR = SLOTS * DH
VW = DH + 1

E, F = 8, 688
TILES = (2 * T) // P + E - 1
FH = F // 2
FC = (F + P - 1) // P
FR = F - (FC - 1) * P


class Step:

    def __init__(self, i, c):
        self.i, self.c = i, c

    def __add__(self, k):
        return Step(self.i, self.c + k)

    def __sub__(self, k):
        return Step(self.i, self.c - k)

    @property
    def n(self):
        return 2 * self.i + self.c

    @property
    def half(self):
        return self.i + self.c // 2

    @property
    def par(self):
        return self.c % 2


def wait(eng, sem, count):
    if not isinstance(count, int) or count > 0:
        eng.wait_ge(sem, count)


def stand(eng, waits_met):
    eng.sem_inc(waits_met, 1)


def self_attention(nc, ps, ident, x, xT, wqT, wqkvT, bqk, bqkv, wop, w2T, b2, wg, wu, WG, WU, load_experts, x1d, x1Td):
    with ExitStack() as ctx:
        def sb(name, shape, dt=F32):
            return ctx.enter_context(nc.sbuf_tensor(name, shape, dt))

        def sem(name):
            return ctx.enter_context(nc.semaphore(name))

        L2 = 2 * L
        wq_sb = sb("wq_sb", [P, KC, D])
        wqkv_sb = sb("wqkv_sb", [P, KC, 3 * D])
        wop_sb = sb("wop_sb", [64, D])
        w2_sb = sb("w2_sb", [64, 1])
        weff = sb("weff", [P, KC])
        bqk_sb = sb("bqk_sb", [P, 4])
        bv_bc = sb("bv_bc", [L, D])
        b2_bc = sb("b2_bc", [L, 1])
        negb2 = sb("negb2", [L, 1])
        xT_sb = sb("xT_sb", [P, KC, L2])
        x_sb = sb("x_sb", [L, 2, D])
        xb = sb("xb", [L, 2, D])
        qinT = sb("qinT", [P, KC, L2])
        rT = sb("rT", [P, KC, L2])
        qkT = sb("qkT", [P, 4, L2])
        va = sb("va", [L, 2, G, DG + 1])
        dist = sb("dist", [L, L])
        mask = sb("mask", [L, 2, 2, 2, L])
        edx = sb("edx", [L, 2])
        edx1 = sb("edx1", [L, 2])
        sig = sb("sig", [L, 2])
        thr = sb("thr", [L, 2, NW])
        s2 = sb("s2", [L, 2, G, L])
        mx = sb("mx", [L, 2, G])
        pr = sb("pr", [L, 2, G * L])
        prT = sb("prT", [L, 2, G * L])
        rc = sb("rc", [L, 2, G, 1])
        o = sb("o", [L, 2, D])
        xr = sb("xr", [L, 2, D])
        stats = sb("stats", [L, 2, 6])
        mv = sb("mv", [L, 2, 2])
        ve = sb("ve", [L, 2])
        rstd = sb("rstd", [L, 2])
        mhalf = sb("mhalf", [L, 2])
        x1 = sb("x1", [L, 2, D])
        x1T = sb("x1T", [P, 2, KC, L])

        w_in = sem("w_in")
        xT_in, x_in = sem("xT_in"), sem("x_in")
        wts_in = sem("wts_in")
        id_set, consts = sem("id_set"), sem("consts")
        weff_mm, weff_ev = sem("weff_mm"), sem("weff_ev")
        xb_ok = sem("xb_ok")
        q_mm, q_ev, r_ok = sem("q_mm"), sem("q_ev"), sem("r_ok")
        qk_mm, qk_ev = sem("qk_mm"), sem("qk_ev")
        v_mm, v_ev = sem("v_mm"), sem("v_ev")
        dx_mm, dx_ev, thr_step, mask_ok = sem("dx_mm"), sem("dx_ev"), sem("thr_step"), sem("mask_ok")
        s_mm, s2_step, s2_ok, p_ok = sem("s_mm"), sem("s2_step"), sem("s2_ok"), sem("p_ok")
        pT_mm, pT_ev, pv_mm, rc_ok, pv_rd = sem("pT_mm"), sem("pT_ev"), sem("pv_mm"), sem("rc_ok"), sem("pv_rd")
        xr_ok, st_ok, mv_ok, ve_ok, rstd_ok, x1_ok = (sem("xr_ok"), sem("st_ok"), sem("mv_ok"), sem("ve_ok"),
                                                      sem("rstd_ok"), sem("x1_ok"))
        xT_mm, xT_ev = sem("xT_mm"), sem("xT_ev")
        x1_out, x1T_out = sem("x1_out"), sem("x1T_out")
        dve_stands, pool_stands = sem("dve_stands"), sem("pool_stands")

        B_QIN, B_QK, B_V, B_S, B_PV = 0, 1, 3, 4, 6
        N_W = 8 * 16

        with nc.Block() as block:

            @block.sync
            def _(sp):
                def load_xT(g):
                    sp.dma_start(xT_sb[:, :, :], xT[:, :, bass.ds(g * L2, L2)]).then_inc(xT_in, 16)

                def load_x(g):
                    sp.dma_start(x_sb[:, :, :], x[bass.ds(2 * g, 2), :, :].rearrange("u l d -> l u d")).then_inc(x_in, 16)

                sp.dma_start(wq_sb[:, :, :], wqT).then_inc(w_in, 16)
                load_xT(0)
                sp.dma_start(wqkv_sb[:, :, :], wqkvT).then_inc(w_in, 16)
                load_x(0)
                sp.dma_start(wop_sb[:, :], wop).then_inc(w_in, 16)
                sp.dma_start(w2_sb[:, :], w2T).then_inc(w_in, 16)
                sp.dma_start(bqk_sb[:, :], bqk).then_inc(w_in, 16)
                sp.dma_start(bv_bc[:, :], bqkv[2 * D:3 * D].partition_broadcast(L)).then_inc(w_in, 16)
                sp.dma_start(b2_bc[:, :], b2.partition_broadcast(L)).then_inc(w_in, 16)

                def step(g, first=False, last=False):
                    if not last:
                        sp.wait_ge(q_mm, g + 1)
                        load_xT(g + 1)
                        sp.wait_ge(xb_ok, g + 1)
                        load_x(g + 1)
                    if not first:
                        store(g - 1)

                def store(g):
                    sp.wait_ge(x1_ok, g + 1)
                    sp.dma_start(x1d[bass.ds(2 * g, 2), :, :].rearrange("u l d -> l u d"), x1[:, :, :]).then_inc(x1_out, 16)
                    sp.wait_ge(xT_ev, g + 1)
                    sp.dma_start(x1Td[bass.ds(2 * g, 2), :, :, :].rearrange("u p k l -> p u k l"),
                                 x1T[:, :, :, :]).then_inc(x1T_out, 16)

                step(0, first=True)
                with sp.Fori(1, PAIRS - 1) as g:
                    step(g)
                step(PAIRS - 1, last=True)
                store(PAIRS - 1)
                sp.wait_ge(x1_out, 16 * PAIRS)
                sp.wait_ge(x1T_out, 16 * PAIRS)

            @block.gpsimd
            def _(pool):
                mask4 = mask[:, :, :, :, :].rearrange("p a u b l -> p a (u b) l")
                pool.memset(ident[:, :], 0.0).then_inc(id_set, 1)
                pool.wait_ge(id_set, 1)
                pool.affine_select(out=ident[:, :], in_=ident[:, :], compare_op=ALU.not_equal, fill=1.0, base=0,
                                   pattern=[[-1, P]], channel_multiplier=1).then_inc(consts, 1)
                pool.iota(dist[:, :], pattern=[[1, L]], base=0, channel_multiplier=-1,
                          allow_small_or_imprecise_dtypes=True).then_inc(id_set, 1)
                pool.memset(mask4, 0.0).then_inc(id_set, 1)
                pool.memset(va[:, :, :, DG:DG + 1], 1.0).then_inc(consts, 1)
                pool.memset(mhalf[:, :], -0.5).then_inc(consts, 1)
                pool.wait_ge(id_set, 3)
                pool.affine_select(out=dist[:, :], in_=dist[:, :], compare_op=ALU.is_ge, fill=BIG, base=0,
                                   pattern=[[1, L]], channel_multiplier=-1).then_inc(consts, 1)
                pool.affine_select(out=mask4, in_=mask4, compare_op=ALU.is_ge, fill=-BIG, base=0,
                                   pattern=[[0, 2], [0, 4], [1, L]], channel_multiplier=-1).then_inc(consts, 1)
                pool.wait_ge(w_in, 16 * 8 - 16)
                pool.tensor_scalar_mul(negb2[:, :], b2_bc[:, :], -1.0).then_inc(consts, 1)

                def add_bias(g):
                    pool.wait_ge(x_in, 16 * (g + 1))
                    wait(pool, xr_ok, 2 * g)
                    pool.tensor_tensor(xb[:, :, :], x_sb[:, :, :],
                                       bv_bc[:, :].unsqueeze(1).to_broadcast([L, 2, D]), ALU.add).then_inc(xb_ok, 1)

                def rstd_of(g):
                    pool.wait_ge(mv_ok, 2 * g + 2)
                    stand(pool, pool_stands)
                    pool.tensor_scalar(ve[:, :], mv[:, :, 1], EPS, None, ALU.add).then_inc(ve_ok, 1)
                    pool.wait_ge(ve_ok, g + 1)
                    pool.tensor_tensor(rstd[:, :], ve[:, :], mhalf[:, :], ALU.pow).then_inc(rstd_ok, 1)

                add_bias(0)
                with pool.Fori(1, PAIRS) as g:
                    add_bias(g)
                    rstd_of(g - 1)
                rstd_of(PAIRS - 1)

            @block.tensor
            def _(pe):
                pe.wait_ge(w_in, N_W - 16)
                for k in range(KC):
                    mm = pe.matmul(ps[:, B_PV, k:k + 1], wop_sb[:, k * P:(k + 1) * P], w2_sb[:, :], start=True, stop=True)
                mm.then_inc(weff_mm, 1)
                pe.wait_ge(consts, 6)

                def q_in(g):
                    pe.wait_ge(xT_in, 16 * (g + 1))
                    wait(pe, dx_ev, g)
                    for m in range(KC):
                        for k in range(KC):
                            mm = pe.matmul(ps[:, B_QIN, m * L2:(m + 1) * L2], wq_sb[:, k, m * P:(m + 1) * P],
                                           xT_sb[:, k, :], start=(k == 0), stop=(k == KC - 1))
                    mm.then_inc(q_mm, 1)

                def qk(g, half):
                    if half == 0:
                        pe.wait_ge(q_ev, g + 1)
                    wait(pe, qk_ev, 2 * g)
                    for m in range(2):
                        c = 2 * half + m
                        for k in range(KC):
                            mm = pe.matmul(ps[:, B_QK + half, m * L2:(m + 1) * L2], wqkv_sb[:, k, c * P:(c + 1) * P],
                                           qinT[:, k, :], start=(k == 0), stop=(k == KC - 1))
                    mm.then_inc(qk_mm, 1)

                def values(g):
                    wait(pe, xT_ev, g - 1)
                    for u in range(2):
                        for k in range(KC):
                            mm = pe.matmul(ps[0:L, B_V, u * D:(u + 1) * D], qinT[:, k, u * L:(u + 1) * L],
                                           wqkv_sb[:, k, 2 * D:3 * D], start=(k == 0), stop=(k == KC - 1))
                    mm.then_inc(v_mm, 1)

                def learned_window(g):
                    pe.wait_ge(r_ok, g + 1)
                    for u in range(2):
                        for k in range(KC):
                            mm = pe.matmul(ps[0:L, B_QIN, 2 * L2 + u:2 * L2 + u + 1], rT[:, k, u * L:(u + 1) * L],
                                           weff[:, k:k + 1], start=(k == 0), stop=(k == KC - 1))
                    mm.then_inc(dx_mm, 1)

                def scores(g, first):
                    pe.wait_ge(qk_ev, 2 * g + 2)
                    if not first:
                        pe.wait_ge(pT_ev, 2 * g)
                    for c in range(4):
                        u, hh = c // 2, c % 2
                        for hp in range(2):
                            r = DG * hp
                            mm = pe.matmul(ps[0:L, B_S + hp, c * L:(c + 1) * L], qkT[r:r + DG, hh, u * L:(u + 1) * L],
                                           qkT[r:r + DG, 2 + hh, u * L:(u + 1) * L], start=True, stop=True)
                            if c == 3:
                                mm.then_inc(s_mm, 1)

                def turn_probs(g):
                    for hp in range(2):
                        pe.wait_ge(p_ok, 2 * g + hp + 1)
                        for c in range(4):
                            mm = pe.transpose(ps[0:L, B_S + hp, c * L:(c + 1) * L], pr[:, hp, c * L:(c + 1) * L],
                                              ident[0:L, 0:L])
                        mm.then_inc(pT_mm, 1)

                def weigh_values(g):
                    pe.wait_ge(pT_ev, 2 * g + 2)
                    pe.wait_ge(v_ev, g + 1)
                    wait(pe, pv_rd, 2 * g)
                    for u in range(2):
                        for h in range(G):
                            mm = pe.matmul(ps[0:L, B_PV + u, h * (DG + 1):(h + 1) * (DG + 1)],
                                           prT[:, h % 2, (2 * u + h // 2) * L:(2 * u + h // 2 + 1) * L],
                                           va[:, u, h, :], start=True, stop=True)
                        mm.then_inc(pv_mm, 1)

                def turn_x1(g, last):
                    pe.wait_ge(x1_ok, g + 1)
                    if not last:
                        pe.wait_ge(v_ev, g + 2)
                    for u in range(2):
                        for k in range(KC):
                            c = u * KC + k
                            mm = pe.transpose(ps[:, B_V, c * L:(c + 1) * L], x1[:, u, k * P:(k + 1) * P],
                                              ident[0:L, 0:L])
                    mm.then_inc(xT_mm, 1)

                q_in(0)
                qk(0, 0)
                qk(0, 1)
                values(0)
                pe.wait_ge(weff_ev, 1)
                learned_window(0)
                scores(0, True)
                with pe.Fori(1, PAIRS) as g:
                    q_in(g)
                    turn_probs(g - 1)
                    qk(g, 0)
                    weigh_values(g - 1)
                    qk(g, 1)
                    values(g)
                    learned_window(g)
                    scores(g, False)
                    turn_x1(g - 1, False)
                turn_probs(PAIRS - 1)
                weigh_values(PAIRS - 1)
                turn_x1(PAIRS - 1, True)

            @block.scalar
            def _(act):
                load_experts(act, WG, wg, WU, wu, wts_in)
                act.wait_ge(weff_mm, 1)
                act.activation(weff[:, :], ps[:, B_PV, 0:KC], ACT.Copy).then_inc(weff_ev, 1)
                act.wait_ge(w_in, N_W - 16)
                act.wait_ge(consts, 6)

                def projections(g):
                    act.wait_ge(q_mm, g + 1)
                    act.activation(qinT[:, :, :], ps[:, B_QIN, 0:2 * L2].rearrange("p (m t) -> p m t", m=KC),
                                   ACT.Copy).then_inc(q_ev, 1)

                def probs_out(g):
                    for u in range(2):
                        act.wait_ge(pT_mm, 2 * g + u + 1)
                        act.activation(prT[:, u, :], ps[0:L, B_S + u, 0:G * L], ACT.Copy).then_inc(pT_ev, 1)

                def qkv_out(g):
                    for half in range(2):
                        act.wait_ge(qk_mm, 2 * g + half + 1)
                        for m in range(2):
                            c = 2 * half + m
                            cp = act.activation(qkT[:, c, :], ps[:, B_QK + half, m * L2:(m + 1) * L2], ACT.Identity,
                                                bias=bqk_sb[:, c:c + 1])
                        cp.then_inc(qk_ev, 1)
                    act.wait_ge(v_mm, g + 1)
                    act.activation(va[:, :, :, 0:DG], ps[0:L, B_V, :].rearrange("p (u h d) -> p u h d", u=2, h=G),
                                   ACT.Copy).then_inc(v_ev, 1)
                    act.wait_ge(dx_mm, g + 1)
                    wait(act, thr_step, 2 * g)
                    act.activation(edx[:, :], ps[0:L, B_QIN, 2 * L2:2 * L2 + 2], ACT.Exp, bias=negb2[:, 0:1],
                                   scale=-1.0).then_inc(dx_ev, 1)

                def exps(g):
                    for u in range(2):
                        act.wait_ge(s2_ok, 2 * g + u + 1)
                        act.activation(pr[:, u, :], s2[:, u, :, :].rearrange("p h l -> p (h l)"),
                                       ACT.Exp).then_inc(p_ok, 1)

                def x1T_copy(g):
                    act.wait_ge(xT_mm, g + 1)
                    wait(act, x1T_out, 16 * g)
                    act.activation(x1T[:, :, :, :],
                                   ps[:, B_V, 0:2 * KC * L].rearrange("p (u k l) -> p u k l", u=2, k=KC),
                                   ACT.Copy).then_inc(xT_ev, 1)

                projections(0)
                qkv_out(0)
                exps(0)
                with act.Fori(1, PAIRS) as g:
                    projections(g)
                    probs_out(g - 1)
                    qkv_out(g)
                    exps(g)
                    x1T_copy(g - 1)
                probs_out(PAIRS - 1)
                x1T_copy(PAIRS - 1)
                act.wait_ge(wts_in, 16 * 2 * E)

            @block.vector
            def _(dve):
                dve.wait_ge(consts, 6)

                def relu(g):
                    dve.wait_ge(q_ev, g + 1)
                    wait(dve, dx_mm, g)
                    dve.tensor_scalar(rT[:, :, :], qinT[:, :, :], 0.0, None, ALU.max).then_inc(r_ok, 1)

                def normalise(g):
                    for u in range(2):
                        pv = ps[0:L, B_PV + u, 0:G * (DG + 1)].rearrange("p (h w) -> p h w", h=G)
                        dve.wait_ge(pv_mm, 2 * g + u + 1)
                        dve.reciprocal(rc[:, u, :, :], pv[:, :, DG:DG + 1]).then_inc(rc_ok, 1)
                        dve.wait_ge(rc_ok, 2 * g + u + 1)
                        dve.tensor_tensor(o[:, u, :].rearrange("p (h d) -> p h d", h=G), pv[:, :, 0:DG],
                                          rc[:, u, :, :].to_broadcast([L, G, DG]), ALU.mult).then_inc(pv_rd, 1)
                        dve.wait_ge(pv_rd, 2 * g + u + 1)
                        dve.wait_ge(xb_ok, g + 1)
                        dve.tensor_tensor(xr[:, u, :], o[:, u, :], xb[:, u, :], ALU.add).then_inc(xr_ok, 1)
                        dve.wait_ge(xr_ok, 2 * g + u + 1)
                        dve.bn_stats(stats[:, u, :], xr[:, u, :]).then_inc(st_ok, 1)
                        dve.wait_ge(st_ok, 2 * g + u + 1)
                        if u == 0:
                            wait(dve, rstd_ok, g)
                        stand(dve, dve_stands)
                        dve.bn_aggr(mv[:, u, :], stats[:, u, :]).then_inc(mv_ok, 1)

                def apply(g):
                    dve.wait_ge(rstd_ok, g + 1)
                    wait(dve, x1_out, 16 * g)
                    wait(dve, xT_mm, g)
                    for u in range(2):
                        ap = dve.tensor_scalar(x1[:, u, :], xr[:, u, :], mv[:, u, 0:1], rstd[:, u:u + 1],
                                               ALU.subtract, ALU.mult)
                    ap.then_inc(x1_ok, 1)

                def masks(g):
                    dve.wait_ge(dx_ev, g + 1)
                    dve.tensor_scalar(edx1[:, :], edx[:, :], 1.0, None, ALU.add).then_inc(thr_step, 1)
                    dve.wait_ge(thr_step, 2 * g + 1)
                    dve.reciprocal(sig[:, :], edx1[:, :]).then_inc(thr_step, 1)
                    dve.wait_ge(thr_step, 2 * g + 2)
                    for w in range(NW):
                        th = dve.tensor_scalar(thr[:, :, w], sig[:, :], float(L), WINDOWS[w], ALU.mult, ALU.add)
                    th.then_inc(mask_ok, 1)
                    dve.wait_ge(mask_ok, 2 * g + 1)
                    for u in range(2):
                        for w in range(NW):
                            mk = dve.tensor_scalar(mask[:, w, u, 0, :], dist[:, :], thr[:, u, w:w + 1], -BIG,
                                                   ALU.is_gt, ALU.mult)
                    mk.then_inc(mask_ok, 1)

                def softmax_in(g):
                    for hp in range(2):
                        n = 2 * g + hp
                        if hp == 0:
                            dve.wait_ge(mask_ok, 2 * g + 2)
                        dve.wait_ge(s_mm, n + 1)
                        wait(dve, p_ok, n - 1)
                        dve.scalar_tensor_tensor(out=s2[:, hp, :, :],
                                                 in0=ps[0:L, B_S + hp, 0:G * L].rearrange("p (h l) -> p h l", h=G),
                                                 scalar=2.0 * float(np.float32(1.0 / np.sqrt(L))),
                                                 in1=mask[:, hp, :, :, :].rearrange("p u b l -> p (u b) l"), op0=ALU.mult, op1=ALU.add).then_inc(s2_step, 1)
                        dve.wait_ge(s2_step, 2 * n + 1)
                        dve.tensor_reduce(mx[:, hp, :], s2[:, hp, :, :], AX_X, ALU.max).then_inc(s2_step, 1)
                        dve.wait_ge(s2_step, 2 * n + 2)
                        dve.tensor_tensor(s2[:, hp, :, :], s2[:, hp, :, :],
                                          mx[:, hp, :].unsqueeze(2).to_broadcast([L, G, L]),
                                          ALU.subtract).then_inc(s2_ok, 1)

                relu(0)
                masks(0)
                softmax_in(0)
                with dve.Fori(1, PAIRS) as g:
                    relu(g)
                    normalise(g - 1)
                    masks(g)
                    apply(g - 1)
                    softmax_in(g)
                normalise(PAIRS - 1)
                apply(PAIRS - 1)


def cross_attention(nc, ps, ident, ctxT, wqT, wkT, wvT, woT, bqk, bv, bo, ws, x1d, x1Td, x2d, accd, LG):
    with ExitStack() as ctx:
        def sb(name, shape, dt=F32):
            return ctx.enter_context(nc.sbuf_tensor(name, shape, dt))

        def sem(name):
            return ctx.enter_context(nc.semaphore(name))

        HH = H // 2
        MR = PARTS * HH
        VC = 32
        HG = P // VC
        NG = H // HG
        wq_sb = sb("cwq_sb", [P, KC, D])
        wk_sb = sb("cwk_sb", [P, KC, D])
        wv_sb = sb("cwv_sb", [P, KC, D])
        wo_sb = sb("cwo_sb", [P, KC, D])
        ws_sb = sb("ws_sb", [P, KC, E])
        bqk_sb = sb("cbqk_sb", [P, 2 * KC])
        bq4 = sb("bq4", [P, KC])
        bv_sb = sb("cbv_sb", [P, KC])
        bvr = sb("bvr", [P, KC, L])
        cbc = sb("cbc", [L, D])
        bo_bc = sb("bo_bc", [L, D])
        negid = sb("negid", [L, L], BF16)
        mhalf = sb("mhalf2", [L, 1])
        cx = [sb(f"cx{u}", [P, KC, CTX]) for u in range(2)]
        x1T_sb = sb("x1T_sb", [P, KC, L])
        x1_sb = sb("x1_sb", [L, D])
        x1b = sb("x1b", [L, D])
        kf = sb("kf", [P, KC, KQ])
        rf = sb("rf", [P, KC, KQ])
        parts = [sb(f"parts{u}", [P, KC, SLOTS, KQ], BF16) for u in range(2)]
        st = [sb(f"st{u}", [SR + MR, H, KQ], BF16) for u in range(2)]
        own = sb("own", [SR + MR, H])
        va = [sb(f"va{u}", [CM, NCH, H, VC]) for u in range(2)]
        pr = sb("cpr", [CM, 2 * HG, NCH * L])
        oT = sb("oT", [P, NG, L])
        mx = sb("cmx", [L, 2, HH])
        mxr = sb("mxr", [L, 2, HH])
        mxp = sb("mxp", [L, 2, SR + MR], BF16)
        rc = sb("crc", [L, H, 1])
        at = sb("at", [L, D])
        atT = sb("atT", [P, KC, L])
        xr = sb("cxr", [L, D])
        stats = sb("cstats", [L, 6])
        mv = sb("cmv", [L, 2])
        ve = sb("cve", [L, 1])
        rstd = sb("crstd", [L, 1])
        x2 = sb("x2", [L, D])
        x2T = sb("x2T", [P, KC, L])

        names = ("w_in id_ok ones_set c_step c_mm c_ok kf_set x1T_in x1_in k_mm q_mm k_ev q_ev k1_ok r_ok k2_ok k3_ok own_step own_ok "
                 "v_mm v_ev s_mm max_ok t_mm exp_ok pv_mm oT_ev o_mm rc_ok at_ok aT_mm aT_ev wo_mm x1b_ok wo_rd st_ok mv_ok "
                 "ve_ok rstd_ok x2_ok x2_out x2T_mm x2T_ev lg_mm lg_ev").split()
        (w_in, id_ok, ones_set, c_step, c_mm, c_ok, kf_set, x1T_in, x1_in, k_mm, q_mm, k_ev, q_ev, k1_ok, r_ok, k2_ok,
         k3_ok, own_step, own_ok, v_mm, v_ev, s_mm, max_ok, t_mm, exp_ok, pv_mm, oT_ev, o_mm, rc_ok, at_ok, aT_mm, aT_ev, wo_mm, x1b_ok,
         wo_rd, st_ok, mv_ok, ve_ok, rstd_ok, x2_ok, x2_out, x2T_mm, x2T_ev, lg_mm, lg_ev) = [sem("c_" + n) for n in names]
        dve_stands, pool_stands, sp_stands = sem("c_dve_stands"), sem("c_pool_stands"), sem("c_sp_stands")
        cx_in = [sem(f"cx_in{u}") for u in range(2)]
        kq_in = [sem(f"kq_in{u}") for u in range(2)]
        mxp_step = [sem(f"mxp_step{u}") for u in range(2)]
        mxp_ok = [sem(f"mxp_ok{u}") for u in range(2)]
        mT_mm = [sem(f"mT_mm{u}") for u in range(2)]
        mT_ev = [sem(f"mT_ev{u}") for u in range(2)]

        B_S, B_T, B_O, M0, M1, M2 = 0, 2, 4, 5, 6, 7
        MS = slice(SR, SR + MR)

        def steps(emit, eng):
            def one(b, lo):
                emit(b, 0 <= lo + 2 < NB, 0 <= lo + 1 < NB, 0 <= lo < NB, 0 <= lo - 1 < NB, lo + 3 < NB)

            for b in (-2, -1, 0):
                one(Step(0, b), b)
            with eng.Fori(0, (NB - 4) // 2) as i:
                for c in (1, 2):
                    one(Step(i, c), c)
            for b in range(NB - 3, NB + 1):
                one(Step(0, b), b)

        with nc.Block() as block:

            @block.sync
            def _(sp):
                def load_ctx(b):
                    sp.dma_start(cx[b.par][:, :, :], ctxT[bass.ds(b.n, 1), :, :, :].rearrange("o p k c -> p (o k) c"))\
                        .then_inc(cx_in[b.par], 16)

                def load_x1T(b):
                    sp.dma_start(x1T_sb[:, :, :], x1Td[bass.ds(b.n, 1), :, :, :].rearrange("o p k l -> p (o k) l"))\
                        .then_inc(x1T_in, 16)

                def load_x1(b):
                    sp.dma_start(x1_sb[:, :], x1d[bass.ds(b.n, 1), :, :].rearrange("o l d -> (o l) d")).then_inc(x1_in, 16)

                sp.dma_start(wk_sb[:, :, :], wkT).then_inc(w_in, 16)
                load_ctx(Step(0, 0))
                sp.dma_start(bqk_sb[:, :], bqk).then_inc(w_in, 16)
                sp.dma_start(wq_sb[:, :, :], wqT).then_inc(w_in, 16)
                load_x1T(Step(0, 0))
                load_ctx(Step(0, 1))
                sp.dma_start(wv_sb[:, :, :], wvT).then_inc(w_in, 16)
                sp.dma_start(wo_sb[:, :, :], woT).then_inc(w_in, 16)
                sp.dma_start(ws_sb[:, :, :], ws).then_inc(w_in, 16)
                sp.dma_start(bv_sb[:, :], bv).then_inc(w_in, 16)
                sp.dma_start(bo_bc[:, :], bo.partition_broadcast(L)).then_inc(w_in, 16)

                def stack(b, half):
                    hs = slice(half * HH, (half + 1) * HH)
                    src = parts[b.par]
                    wait(sp, kq_in[half], 16 * SLOTS * b.n)
                    for s in range(SLOTS):
                        sp.dma_start(st[b.par][s * DH:(s + 1) * DH, hs, :], src[:, half, s, :]).then_inc(kq_in[half], 16)

                def emit(b, kq, s, t, tail, more):
                    if kq and more:
                        sp.wait_ge(q_mm, b.n + 3)
                        load_x1T(b + 3)
                    if kq:
                        sp.wait_ge(k3_ok, 2 * b.n + 5)
                        stand(sp, sp_stands)
                        wait(sp, t_mm, H * b.n + HH)
                        stand(sp, sp_stands)
                        stack(b + 2, 0)
                    if s and more:
                        sp.wait_ge(v_mm, 2 * b.n + 4)
                        stand(sp, sp_stands)
                        load_ctx(b + 3)
                    if t:
                        wait(sp, x1b_ok, b.n)
                        load_x1(b)
                    if tail:
                        sp.wait_ge(x2_ok, b.n)
                        for dst in (x2d, accd):
                            sp.dma_start(dst[bass.ds((b.n - 1) * L, L), :], x2[:, :]).then_inc(x2_out, 16)
                    if kq:
                        sp.wait_ge(k3_ok, 2 * b.n + 6)
                        stand(sp, sp_stands)
                        wait(sp, t_mm, H * b.n + H)
                        stand(sp, sp_stands)
                        stack(b + 2, 1)

                steps(emit, sp)
                sp.wait_ge(x2_out, 32 * NB)

            @block.gpsimd
            def _(pool):
                pool.memset(own[MS, :], 0.0).then_inc(own_step, 1)
                for r in range(PARTS):
                    pool.wait_ge(own_step, r + 1)
                    o = own[MS, :].rearrange("p (u h) -> p u h", u=2)
                    sel = pool.affine_select(out=o, in_=o, compare_op=ALU.not_equal, fill=1.0, base=-r * HH,
                                             pattern=[[0, 2], [-1, HH]], channel_multiplier=1)
                    sel.then_inc(own_step if r < PARTS - 1 else own_ok, 1)
                pool.wait_ge(own_ok, 1)
                for u in range(2):
                    pool.memset(va[u][:, :, :, DH:VC], 1.0).then_inc(ones_set, 1)
                pool.memset(mhalf[:, :], -0.5).then_inc(ones_set, 1)
                pool.memset(mxp[:, :, 0:SR], 0.0).then_inc(ones_set, 1)
                pool.tensor_scalar_mul(negid[:, :], ident[0:L, 0:L], -1.0).then_inc(ones_set, 1)

                def part(half, r):
                    return mxp[:, half, SR + r * HH:SR + (r + 1) * HH]

                def split_maximum(b, half):
                    pool.wait_ge(max_ok, H * b.n + HH * (half + 1))
                    wait(pool, mT_mm[half], b.n)
                    stand(pool, pool_stands)
                    pool.tensor_copy(part(half, 0), mx[:, half, :]).then_inc(mxp_step[half], 1)
                    pool.wait_ge(mxp_step[half], 3 * b.n + 1)
                    pool.tensor_tensor(mxr[:, half, :], mx[:, half, :], part(half, 0),
                                       ALU.subtract).then_inc(mxp_step[half], 1)
                    pool.wait_ge(mxp_step[half], 3 * b.n + 2)
                    stand(pool, pool_stands)
                    pool.tensor_copy(part(half, 1), mxr[:, half, :]).then_inc(mxp_step[half], 1)
                    pool.wait_ge(mxp_step[half], 3 * b.n + 3)
                    pool.tensor_tensor(part(half, 2), mxr[:, half, :], part(half, 1),
                                       ALU.subtract).then_inc(mxp_ok[half], 1)

                def emit(b, kq, s, t, tail, more):
                    if t:
                        split_maximum(b, 1)
                    if tail:
                        pool.wait_ge(x1_in, 16 * b.n)
                        wait(pool, wo_rd, b.n - 1)
                        pool.wait_ge(c_ok, 1)
                        pool.tensor_tensor(x1b[:, :], x1_sb[:, :], cbc[:, :], ALU.add).then_inc(x1b_ok, 1)
                    if s:
                        split_maximum(b + 1, 0)
                    if tail:
                        pool.wait_ge(mv_ok, b.n)
                        stand(pool, pool_stands)
                        pool.tensor_scalar(ve[:, :], mv[:, 1:2], EPS, None, ALU.add).then_inc(ve_ok, 1)
                        pool.wait_ge(ve_ok, b.n)
                        pool.tensor_tensor(rstd[:, :], ve[:, :], mhalf[:, :], ALU.pow).then_inc(rstd_ok, 1)

                steps(emit, pool)

            @block.tensor
            def _(pe):
                pe.wait_ge(w_in, 16 * 8)
                pe.wait_ge(ones_set, 5)
                pe.wait_ge(c_step, 2)
                for k in range(KC):
                    mm = pe.matmul(ps[0:L, B_O, 0:D], bvr[:, k, :], wo_sb[:, k, :], start=(k == 0), stop=(k == KC - 1))
                mm.then_inc(c_mm, 1)
                pe.wait_ge(c_ok, 1)

                def query_scores(b, h):
                    half, hh = divmod(h, HH)
                    if hh == 0:
                        pe.wait_ge(kq_in[half], 16 * SLOTS * (b.n + 1))
                    wait(pe, max_ok, H * b.n + h - 1)
                    pe.matmul(ps[0:L, B_S + h % 2, 0:CTX], st[b.par][0:SR, h, CTX:KQ], st[b.par][0:SR, h, 0:CTX],
                              start=True, stop=True).then_inc(s_mm, 1)

                def key_scores(b, h):
                    half, hh = divmod(h, HH)
                    if hh == 0:
                        pe.wait_ge(mT_ev[half], b.n + 1)
                    wait(pe, exp_ok, H * b.n + h - 1)
                    for c in range(NCH):
                        mm = pe.matmul(ps[0:CM, B_T + h % 2, c * L:(c + 1) * L],
                                       st[b.par][:, h, c * CH:c * CH + CM], st[b.par][:, h, CTX:KQ],
                                       start=True, stop=True)
                    mm.then_inc(t_mm, 1)

                def weigh_values(b, g):
                    pe.wait_ge(exp_ok, H * b.n + HG * (g + 1))
                    if g == 0:
                        wait(pe, oT_ev, b.n)
                        pe.wait_ge(v_ev, 2 * b.n + 2)
                    for c in range(NCH):
                        n = CH if c < NCH - 1 else CM
                        for j in range(HG):
                            h = HG * g + j
                            mm = pe.matmul(ps[j * VC:(j + 1) * VC, B_O, g * L:(g + 1) * L], va[b.par][0:n, c, h, :],
                                           pr[0:n, h % (2 * HG), c * L:(c + 1) * L], start=(c == 0), stop=(c == NCH - 1))
                    mm.then_inc(pv_mm, 1)

                def turn_maximum(b, half):
                    pe.wait_ge(mxp_ok[half], b.n + 1)
                    bank = M1
                    if half == 0:
                        pe.wait_ge(v_ev, 2 * b.n + 1)
                    else:
                        bank = M2
                        wait(pe, lg_ev, b.n - 1)
                    pe.matmul(ps[0:SR + MR, bank, 0:L], mxp[:, half, :],
                              negid[:, :], start=True, stop=True).then_inc(mT_mm[half], 1)

                def keys(b, m):
                    if m == 0:
                        pe.wait_ge(cx_in[b.par], 16 * (b.half + 1))
                        wait(pe, x2T_ev, b.n - 3)
                    else:
                        wait(pe, mT_ev[0], b.n - 1)
                    for k in range(KC):
                        mm = pe.matmul(ps[:, M0 + m, 0:CTX], wk_sb[:, k, m * P:(m + 1) * P], cx[b.par][:, k, :],
                                       start=(k == 0), stop=(k == KC - 1))
                    mm.then_inc(k_mm, 1)

                def queries(b):
                    pe.wait_ge(x1T_in, 16 * (b.n + 1))
                    wait(pe, mT_ev[1], b.n - 1)
                    for m in range(KC):
                        for k in range(KC):
                            mm = pe.matmul(ps[:, M2, m * L:(m + 1) * L], wq_sb[:, k, m * P:(m + 1) * P],
                                           x1T_sb[:, k, :], start=(k == 0), stop=(k == KC - 1))
                    mm.then_inc(q_mm, 1)

                def values(b, c):
                    bank, o = (M1, c * D) if c < 2 else (M2, 0)
                    for k in range(KC):
                        mm = pe.matmul(ps[0:CM, bank, o:o + D], cx[b.par][:, k, c * CH:c * CH + CM], wv_sb[:, k, :],
                                       start=(k == 0), stop=(k == KC - 1))
                    if c > 0:
                        mm.then_inc(v_mm, 1)

                def emit(b, kq, s, t, tail, more):
                    for h in range(H):
                        if s:
                            query_scores(b + 1, h)
                        if t:
                            key_scores(b, h)
                        if h == 0:
                            if tail:
                                weigh_values(b - 1, NG - 1)
                            if kq:
                                keys(b + 2, 0)
                        if h == 0 and t:
                            turn_maximum(b, 1)
                        if h == 1 and kq:
                            keys(b + 2, 1)
                        if h == 2 and kq:
                            queries(b + 2)
                        if h == 2 and tail:
                            pe.wait_ge(oT_ev, b.n)
                            if kq:
                                pe.wait_ge(k_ev, 2 * b.n + 5)
                            for g in range(NG):
                                mm = pe.transpose(ps[0:L, M0, g * P:(g + 1) * P], oT[:, g, :], ident[:, :])
                            mm.then_inc(o_mm, 1)
                        if h == 4 and tail:
                            pe.wait_ge(at_ok, b.n)
                            for k in range(KC):
                                mm = pe.transpose(ps[:, M0, k * L:(k + 1) * L], at[:, k * P:(k + 1) * P], ident[0:L, 0:L])
                            mm.then_inc(aT_mm, 1)
                        if h == 5 and s:
                            pe.wait_ge(k_ev, 2 * b.n + 6 if kq else 2 * NB)
                            if b.c >= 0:
                                wait(pe, mT_ev[0], b.n + 1)
                            if b.c == -1:
                                pe.wait_ge(cx_in[0], 16)
                            values(b + 1, 0)
                        if h == 7 and s:
                            values(b + 1, 1)
                        if h == 9 and s:
                            if kq:
                                pe.wait_ge(q_ev, b.n + 3)
                            elif t:
                                pe.wait_ge(mT_ev[1], b.n + 1)
                            values(b + 1, 2)
                        if h == 6 and tail:
                            pe.wait_ge(aT_ev, b.n)
                            for k in range(KC):
                                mm = pe.matmul(ps[0:L, M0, 0:D], atT[:, k, :], wo_sb[:, k, :],
                                               start=(k == 0), stop=(k == KC - 1))
                            mm.then_inc(wo_mm, 1)
                        if h == 12 and tail:
                            pe.wait_ge(x2_ok, b.n)
                            for k in range(KC):
                                mm = pe.transpose(ps[:, M0, k * L:(k + 1) * L], x2[:, k * P:(k + 1) * P], ident[0:L, 0:L])
                            mm.then_inc(x2T_mm, 1)
                        if h == 11 and s:
                            turn_maximum(b + 1, 0)
                        if h == 14 and tail:
                            pe.wait_ge(x2T_ev, b.n)
                            if s:
                                pe.wait_ge(v_ev, 2 * b.n + 4)
                            elif t:
                                pe.wait_ge(mT_ev[1], b.n + 1)
                            for k in range(KC):
                                mm = pe.matmul(ps[0:L, M2, 0:E], x2T[:, k, :], ws_sb[:, k, :],
                                               start=(k == 0), stop=(k == KC - 1))
                            mm.then_inc(lg_mm, 1)
                        if t and h > 0 and h % HG == 0:
                            weigh_values(b, h // HG - 1)

                steps(emit, pe)

            @block.scalar
            def _(act):
                act.wait_ge(w_in, 16 * 8)
                act.wait_ge(ones_set, 5)
                act.mul(bq4[:, :], bqk_sb[:, 0:KC], 1.0 / np.sqrt(DH)).then_inc(c_step, 1)
                act.wait_ge(c_ok, 1)

                def maximum_out(b, half):
                    act.wait_ge(mT_mm[half], b.n + 1)
                    bank = M1 if half == 0 else M2
                    act.activation(st[b.par][MS, half * HH:(half + 1) * HH, CTX:KQ],
                                   ps[MS, bank, 0:L].unsqueeze(1).to_broadcast([MR, HH, L]), ACT.Copy).then_inc(mT_ev[half], 1)

                def keys_out(b, m):
                    act.wait_ge(k_mm, 2 * b.n + m + 1)
                    wait(act, r_ok, 2 * b.n)
                    act.activation(kf[:, m, 0:CTX], ps[:, M0 + m, 0:CTX], ACT.Identity,
                                   bias=bqk_sb[:, KC + m:KC + m + 1]).then_inc(k_ev, 1)

                def emit(b, kq, s, t, tail, more):
                    for h in range(H):
                        if t:
                            act.wait_ge(t_mm, H * b.n + h + 1)
                            if h % HG == 0:
                                wait(act, pv_mm, NG * b.n + h // HG - 1)
                            act.activation(pr[:, h % (2 * HG), :], ps[0:CM, B_T + h % 2, 0:NCH * L], ACT.Exp).then_inc(exp_ok, 1)
                        if h == 0 and kq:
                            keys_out(b + 2, 0)
                        if h == 0 and tail:
                            act.wait_ge(pv_mm, NG * b.n)
                            act.activation(oT[:, :, :], ps[:, B_O, 0:NG * L].rearrange("p (g l) -> p g l", g=NG),
                                           ACT.Copy).then_inc(oT_ev, 1)
                        if h == 0 and t:
                            maximum_out(b, 1)
                        if h == 1 and kq:
                            keys_out(b + 2, 1)
                        if h == 2 and kq:
                            act.wait_ge(q_mm, b.n + 3)
                            for m in range(KC):
                                cp = act.activation(kf[:, m, CTX:KQ], ps[:, M2, m * L:(m + 1) * L], ACT.Identity,
                                                    bias=bq4[:, m:m + 1], scale=1.0 / np.sqrt(DH))
                            cp.then_inc(q_ev, 1)
                        if h == 4 and tail:
                            act.wait_ge(aT_mm, b.n)
                            act.activation(atT[:, :, :], ps[:, M0, 0:KC * L].rearrange("p (k l) -> p k l", k=KC),
                                           ACT.Copy).then_inc(aT_ev, 1)
                        if h in (4, 6) and kq:
                            m = (h - 4) // 2
                            pt = parts[b.par][:, m, :, :]
                            act.wait_ge(k1_ok, 2 * b.n + 5 + m)
                            act.activation(pt[:, 0:3:2, 0:CTX], pt[:, 4:5, 0:CTX].to_broadcast([P, 2, CTX]), ACT.Copy)
                            act.activation(pt[:, 3:6:2, CTX:KQ], pt[:, 4:5, CTX:KQ].to_broadcast([P, 2, L]), ACT.Copy)
                        if h in (5, 7) and kq:
                            m = (h - 5) // 2
                            pt = parts[b.par][:, m, :, :]
                            act.wait_ge(r_ok, 2 * b.n + 5 + m)
                            act.activation(pt[:, 1:4:2, 0:CTX], rf[:, m:m + 1, 0:CTX].to_broadcast([P, 2, CTX]), ACT.Copy)
                            act.activation(pt[:, 1:3, CTX:KQ], rf[:, m:m + 1, CTX:KQ].to_broadcast([P, 2, L]),
                                           ACT.Copy).then_inc(k2_ok, 1)
                        if h == 8 and s:
                            act.wait_ge(v_mm, 2 * b.n + 3)
                            wait(act, pv_mm, NG * b.n)
                            act.activation(va[(b + 1).par][:, 0:2, :, 0:DH],
                                           ps[0:CM, M1, :].rearrange("p (c h d) -> p c h d", c=2, h=H),
                                           ACT.Copy).then_inc(v_ev, 1)
                        if h == 10 and s:
                            act.wait_ge(v_mm, 2 * b.n + 4)
                            act.activation(va[(b + 1).par][:, 2, :, 0:DH],
                                           ps[0:CM, M2, 0:D].rearrange("p (h d) -> p h d", h=H),
                                           ACT.Copy).then_inc(v_ev, 1)
                        if h == 12 and s:
                            maximum_out(b + 1, 0)
                        if h == 13 and tail:
                            act.wait_ge(x2T_mm, b.n)
                            act.activation(x2T[:, :, :], ps[:, M0, 0:KC * L].rearrange("p (k l) -> p k l", k=KC),
                                           ACT.Copy).then_inc(x2T_ev, 1)
                        if h == 14 and tail:
                            act.wait_ge(lg_mm, b.n)
                            act.activation(LG[:, bass.ds(b.n - 1, 1), :], ps[0:L, M2, 0:E].unsqueeze(1),
                                           ACT.Copy).then_inc(lg_ev, 1)

                steps(emit, act)

            @block.vector
            def _(dve):
                dve.wait_ge(w_in, 16 * 8)
                dve.wait_ge(own_ok, 1)
                for u in range(2):
                    dve.tensor_copy(st[u][MS, :, 0:CTX], own[MS, :].unsqueeze(2).to_broadcast([MR, H, CTX]))
                dve.tensor_copy(bvr[:, :, :], bv_sb[:, :].unsqueeze(2).to_broadcast([P, KC, L])).then_inc(c_step, 1)
                dve.wait_ge(c_mm, 1)
                dve.tensor_tensor(cbc[:, :], ps[0:L, B_O, 0:D], bo_bc[:, :], ALU.add).then_inc(c_ok, 1)

                def emit(b, kq, s, t, tail, more):
                    for h in range(H):
                        if s:
                            half, hh = divmod(h, HH)
                            dve.wait_ge(s_mm, H * b.n + H + h + 1)
                            if hh == 0:
                                wait(dve, mxp_ok[half], b.n + 1)
                            dve.tensor_reduce(mx[:, half, hh:hh + 1], ps[0:L, B_S + h % 2, 0:CTX], AX_X,
                                              ALU.max).then_inc(max_ok, 1)
                        if h == 2 and tail:
                            pv = ps[0:L, M0, :].rearrange("p (h w) -> p h w", h=H)
                            dve.wait_ge(o_mm, b.n)
                            dve.reciprocal(rc[:, :, :], pv[:, :, DH:VW]).then_inc(rc_ok, 1)
                            dve.wait_ge(rc_ok, b.n)
                            wait(dve, aT_mm, b.n - 1)
                            dve.tensor_tensor(at[:, :].rearrange("p (h d) -> p h d", h=H), pv[:, :, 0:DH],
                                              rc[:, :, :].to_broadcast([L, H, DH]), ALU.mult).then_inc(at_ok, 1)
                        if h in (3, 5) and kq:
                            m = (h - 3) // 2
                            dve.wait_ge(k_ev, 2 * b.n + 6)
                            dve.wait_ge(q_ev, b.n + 3)
                            wait(dve, kq_in[m], 16 * SLOTS * (b.n + 1))
                            dve.tensor_copy(parts[b.par][:, m, 4, :], kf[:, m, :]).then_inc(k1_ok, 1)
                        if h in (4, 6) and kq:
                            m = (h - 4) // 2
                            dve.wait_ge(k1_ok, 2 * b.n + 5 + m)
                            dve.tensor_tensor(rf[:, m, :], kf[:, m, :], parts[b.par][:, m, 4, :],
                                              ALU.subtract).then_inc(r_ok, 1)
                        if h in (7, 12) and kq:
                            m = (h - 7) // 5
                            dve.wait_ge(k2_ok, 2 * b.n + 5 + m)
                            for slot, one, c in ((5, 3, slice(0, CTX)), (0, 1, slice(CTX, KQ))):
                                k3 = dve.tensor_tensor(parts[b.par][:, m, slot, c], rf[:, m, c], parts[b.par][:, m, one, c],
                                                       ALU.subtract)
                            k3.then_inc(k3_ok, 1)
                        if h == 8 and tail:
                            dve.wait_ge(wo_mm, b.n)
                            dve.wait_ge(x1b_ok, b.n)
                            dve.tensor_tensor(xr[:, :], ps[0:L, M0, 0:D], x1b[:, :], ALU.add).then_inc(wo_rd, 1)
                        if h == 9 and tail:
                            dve.wait_ge(wo_rd, b.n)
                            dve.bn_stats(stats[:, :], xr[:, :]).then_inc(st_ok, 1)
                            dve.wait_ge(st_ok, b.n)
                            wait(dve, rstd_ok, b.n - 1)
                            stand(dve, dve_stands)
                            dve.bn_aggr(mv[:, :], stats[:, :]).then_inc(mv_ok, 1)
                        if h == 11 and tail:
                            dve.wait_ge(rstd_ok, b.n)
                            wait(dve, x2_out, 32 * (b.n - 1))
                            wait(dve, x2T_mm, b.n - 1)
                            dve.tensor_scalar(x2[:, :], xr[:, :], mv[:, 0:1], rstd[:, 0:1],
                                              ALU.subtract, ALU.mult).then_inc(x2_ok, 1)

                steps(emit, dve)


def experts(nc, ps, ident, LG, bs, wd, WG, WU, x2d, accd, out):
    with ExitStack() as ctx:
        def sb(name, shape, dt=F32):
            return ctx.enter_context(nc.sbuf_tensor(name, shape, dt))

        def sem(name):
            return ctx.enter_context(nc.semaphore(name))

        NBH = 2 * NB
        JT = (T + P - 1) // P
        WD = sb("WD", [P, FC, E, D])
        bs_bc = sb("bs_bc", [L, E])
        lg = sb("lg", [L, NB, E])
        best = sb("best", [L, 2, NB])
        eq = sb("eq", [L, NB, E])
        top = sb("top", [L, NB])
        oh = sb("oh", [L, 2, NB, E])
        dm = sb("dm", [L, NB])
        e2 = sb("e2", [L, NB])
        den = sb("den", [L, NB])
        w = sb("w", [L, 2, NB])
        M = sb("M", [L, NB, E])
        pref = sb("pref", [L, E])
        before = sb("before", [L, L])
        ones = sb("ones", [L, L])
        run = [sb(f"run{u}", [L, NB // 2 + NB, E]) for u in range(2)]
        step = sb("step", [L, JT])
        more = sb("more", [L, E, JT])
        off = [sb(f"off{u}", [L, 2 * E]) for u in range(2)]
        off128 = sb("off128", [L, E])
        pos = sb("pos", [L, NB, E])
        posc = sb("posc", [L, 2, NB, E])
        place = sb("place", [L, 2, NB])
        place_i = sb("place_i", [L, 2, NB], I32)
        hi_i = sb("hi_i", [L, NBH], I32)
        lo_i = sb("lo_i", [L, NBH], I32)
        hi = sb("hi", [L, NBH])
        lo = sb("lo", [L, NBH])
        iot = sb("iot", [L, P])
        tok = sb("tok", [L, NB])
        ohl = sb("ohl", [L, NBH, P])
        ohh = sb("ohh", [L, NBH, TILES])
        rh = sb("rh", [L, NBH, 2, TILES])
        inv = sb("inv", [P, TILES])
        pad = sb("pad", [P, TILES])
        spare = sb("spare", [P, 1])
        spare_i = sb("spare_i", [P, 1], I32)
        gat = sb("gat", [P, TILES], I32)
        sca = sb("sca", [P, TILES], I32)
        wt = sb("wt", [P, TILES])
        tex = sb("tex", [L, TILES, E])
        texf = sb("texf", [L, TILES])
        expert_of = sb("expert_of", [L, TILES], I32)

        gi = sb("gi", [P, 2], U32)
        si = sb("si", [P, 2], U32)
        xs = sb("xs", [P, 2, D])
        xsT = sb("xsT", [P, 2, KC, P])
        sg = sb("sg", [P, 2, FH])
        hh = sb("hh", [P, 2, F])
        hT = sb("hT", [P, 2, FC, P])
        y = sb("y", [P, 2, D])

        acc = ohl[:, :, :].rearrange("p n c -> p (n c)").rearrange("p (b d) -> p b d", d=D)
        stats = sb("fstats", [L, NB, 6])
        mv = sb("fmv", [L, NB, 2])
        ve = sb("fve", [L, NB])
        rstd = sb("frstd", [L, NB])
        mhalf = sb("fmhalf", [L, NB])

        names = ("b_in wd_in set_a const chain dm_ok e2_ok M_ok cnt_mm rh_ok inv_mm lists_ok gi_ok si_ok xT_mm xT_ev "
                 "gu_mm sg_ok h_ok hT_mm hTa_ev hTb_ev y_mm y_ok added acc_in mv_ok ve_ok rstd_ok res_ok st_ok out_sent").split()
        (b_in, wd_in, set_a, const, chain, dm_ok, e2_ok, M_ok, cnt_mm, rh_ok, inv_mm, lists_ok, gi_ok, si_ok, xT_mm,
         xT_ev, gu_mm, sg_ok, h_ok, hT_mm, hTa_ev, hTb_ev, y_mm, y_ok, added, acc_in, mv_ok, ve_ok, rstd_ok, res_ok, st_ok,
         out_sent) = [sem("e_" + n) for n in names]
        pool_stands = sem("e_pool_stands")
        xs_in = [sem(f"xs_in{u}") for u in range(2)]
        acc_ins = [sem(f"acc_in{q}") for q in range(4)]

        B_G, B_U, B_H, B_Y, B_X = 0, 2, 4, 6, 7
        N_CONST = 11
        QB = NB // 4

        def steps(emit, eng):
            for t in range(-1, 3):
                emit(Step(0, t), t)
            with eng.Fori(0, (TILES - 6) // 2) as i:
                for c in (3, 4):
                    emit(Step(i, c), c)
            for t in range(TILES - 3, TILES + 1):
                emit(Step(0, t), t)

        with nc.Block() as block:

            @block.sync
            def _(sp):
                sp.dma_start(bs_bc[:, :], bs.partition_broadcast(L)).then_inc(b_in, 16)
                for c in range(FC - 1):
                    sp.dma_start(WD[:, c, :, :], wd[:, c * P:(c + 1) * P, :].rearrange("e p d -> p e d")).then_inc(wd_in, 16)
                sp.dma_start(WD[0:FR, FC - 1, :, :], wd[:, (FC - 1) * P:F, :].rearrange("e p d -> p e d"))\
                    .then_inc(wd_in, 16)
                sp.wait_ge(added, 16 * TILES)
                a = accd.rearrange("(b l) d -> l b d", l=L)
                for q in range(4):
                    sp.dma_start(acc[:, q * QB:(q + 1) * QB, :], a[:, q * QB:(q + 1) * QB, :]).then_inc(acc_ins[q], 16)
                for q in range(4):
                    sp.wait_ge(res_ok, q + 1)
                    sp.dma_start(out[q * QB:(q + 1) * QB, :, :].rearrange("b l d -> l b d"),
                                 acc[:, q * QB:(q + 1) * QB, :]).then_inc(out_sent, 16)
                sp.wait_ge(out_sent, 16 * 4)

            @block.gpsimd
            def _(pool):
                fl = dict(allow_small_or_imprecise_dtypes=True)
                pool.iota(pref[:, :], pattern=[[-1, E]], base=E, channel_multiplier=0, **fl).then_inc(const, 1)
                pool.memset(before[:, :], 1.0).then_inc(set_a, 1)
                pool.memset(ones[:, :], 1.0).then_inc(const, 1)
                for u in range(2):
                    pool.memset(run[u][:, 0:NB // 2, :], 0.0).then_inc(const, 1)
                    pool.memset(off[u][:, 0:E], 0.0).then_inc(const, 1)
                pool.iota(step[:, :], pattern=[[P, JT]], base=0, channel_multiplier=0, **fl).then_inc(const, 1)
                pool.iota(iot[:, :], pattern=[[1, P]], base=0, channel_multiplier=0, **fl).then_inc(const, 1)
                pool.iota(tok[:, :], pattern=[[L, NB]], base=1, channel_multiplier=1, **fl).then_inc(const, 1)
                pool.wait_ge(set_a, 1)
                pool.affine_select(out=before[:, :], in_=before[:, :], compare_op=ALU.is_gt, fill=0.0, base=0,
                                   pattern=[[1, L]], channel_multiplier=-1).then_inc(const, 1)
                pool.wait_ge(const, 10 - 1)
                pool.iota(spare[:, :], pattern=[[0, 1]], base=2 * T + 1, channel_multiplier=1, **fl).then_inc(const, 1)
                pool.wait_ge(const, 10)
                pool.memset(mhalf[:, :], -0.5).then_inc(const, 1)

                def gather(t):
                    wait(pool, xT_mm, t.n - 1)
                    stand(pool, pool_stands)
                    pool.tensor_copy(gi[:, t.par:t.par + 1].bitcast(I32), gat[:, bass.ds(t.n, 1)]).then_inc(gi_ok, 1)
                    pool.wait_ge(gi_ok, t.n + 1)
                    stand(pool, pool_stands)
                    pool.indirect_dma_start(xs[:, t.par, :], None, x2d,
                                            bass.IndirectOffsetOnAxis(ap=gi[:, t.par:t.par + 1], axis=0))\
                        .then_inc(xs_in[t.par], 16)

                def add_rows(t):
                    wait(pool, added, 16 * t.n)
                    stand(pool, pool_stands)
                    pool.tensor_copy(si[:, t.par:t.par + 1].bitcast(I32), sca[:, bass.ds(t.n, 1)]).then_inc(si_ok, 1)
                    pool.wait_ge(si_ok, t.n + 1)
                    pool.wait_ge(y_ok, t.n + 1)
                    stand(pool, pool_stands)
                    pool.indirect_dma_start(accd, bass.IndirectOffsetOnAxis(ap=si[:, t.par:t.par + 1], axis=0),
                                            y[:, t.par, :], None, compute_op=ALU.add, bounds_check=last_token,
                                            oob_is_err=False).then_inc(added, 16)

                pool.wait_ge(lists_ok, 3)
                last_token = pool.to_reg(T - 1)

                def emit(t, n):
                    if n == -1:
                        gather(t + 1)
                    if n + 2 < TILES:
                        gather(t + 2)
                    if n - 1 >= 0:
                        add_rows(t - 1)

                steps(emit, pool)
                for q in range(4):
                    pool.wait_ge(mv_ok, q + 1)
                    s = slice(q * QB, (q + 1) * QB)
                    pool.tensor_scalar(ve[:, s], mv[:, s, 1], EPS, None, ALU.add).then_inc(ve_ok, 1)
                    pool.wait_ge(ve_ok, q + 1)
                    pool.tensor_tensor(rstd[:, s], ve[:, s], mhalf[:, s], ALU.pow).then_inc(rstd_ok, 1)

            @block.tensor
            def _(pe):
                pe.wait_ge(const, N_CONST)
                pe.wait_ge(M_ok, 1)
                Mf = M[:, :, :].rearrange("p b e -> p (b e)")
                pe.matmul(ps[0:L, B_G, 0:NB * E], before[:, :], Mf, start=True, stop=True)
                pe.matmul(ps[0:L, B_G + 1, 0:NB * E], ones[:, :], Mf, start=True, stop=True).then_inc(cnt_mm, 1)
                pe.wait_ge(rh_ok, 1)
                for n in range(NBH):
                    mm = pe.matmul(ps[:, B_Y, 0:2 * TILES], ohl[:, n, :], rh[:, n, :, :].rearrange("p a t -> p (a t)"),
                                   start=(n == 0), stop=(n == NBH - 1))
                mm.then_inc(inv_mm, 1)
                pe.wait_ge(lists_ok, 3)

                def turn_rows(t):
                    pe.wait_ge(xs_in[t.par], 16 * (t.half + 1))
                    wait(pe, xT_ev, t.n)
                    for k in range(KC):
                        mm = pe.transpose(ps[:, B_X, k * P:(k + 1) * P], xs[:, t.par, k * P:(k + 1) * P], ident[:, :])
                    mm.then_inc(xT_mm, 1)

                def gate_up(t):
                    e = pe.value_load(expert_of[0:1, bass.ds(t.n, 1)], min_val=0, max_val=E - 1)
                    pe.wait_ge(xT_ev, t.n + 1)
                    for f in range(2):
                        wait(pe, h_ok, 2 * t.n + f - 1)
                        for bank, W in ((B_G, WG), (B_U, WU)):
                            for k in range(KC):
                                mm = pe.matmul(ps[:, bank + f, 0:FH], xsT[:, t.par, k, :],
                                               W[:, k, bass.ds(e, 1), f * FH:(f + 1) * FH],
                                               start=(k == 0), stop=(k == KC - 1))
                            mm.then_inc(gu_mm, 1)

                def turn_hidden(t):
                    pe.wait_ge(h_ok, 2 * t.n + 2)
                    wait(pe, hTa_ev, t.n)
                    wait(pe, hTb_ev, t.n)
                    for c in range(FC):
                        n = P if c < FC - 1 else FR
                        mm = pe.transpose(ps[0:n, B_H + c // 4, c % 4 * P:(c % 4 + 1) * P],
                                          hh[:, t.par, c * P:c * P + n], ident[:, :])
                        if c in (3, FC - 1):
                            mm.then_inc(hT_mm, 1)

                def down(t):
                    e = pe.value_load(expert_of[0:1, bass.ds(t.n, 1)], min_val=0, max_val=E - 1)
                    wait(pe, y_ok, t.n)
                    for c in range(FC):
                        n = P if c < FC - 1 else FR
                        if c == 0:
                            pe.wait_ge(hTa_ev, t.n + 1)
                        if c == 4:
                            pe.wait_ge(hTb_ev, t.n + 1)
                        mm = pe.matmul(ps[:, B_Y, 0:D], hT[0:n, t.par, c, :], WD[0:n, c, bass.ds(e, 1), :],
                                       start=(c == 0), stop=(c == FC - 1))
                    mm.then_inc(y_mm, 1)

                def emit(t, n):
                    if n >= 1:
                        turn_hidden(t - 1)
                    if n + 1 < TILES:
                        turn_rows(t + 1)
                    if n == 1:
                        pe.wait_ge(wd_in, 16 * FC)
                    if n >= 1:
                        down(t - 1)
                    if n + 1 < TILES:
                        gate_up(t + 1)

                steps(emit, pe)

            @block.scalar
            def _(act):
                act.wait_ge(dm_ok, 1)
                act.activation(e2[:, :], dm[:, :], ACT.Exp).then_inc(e2_ok, 1)

                def rows_out(t):
                    act.wait_ge(xT_mm, t.n + 1)
                    wait(act, gu_mm, 4 * t.n - 4)
                    act.activation(xsT[:, t.par, :, :], ps[:, B_X, 0:KC * P].rearrange("p (k t) -> p k t", k=KC),
                                   ACT.Copy).then_inc(xT_ev, 1)

                def silus(t):
                    for f in range(2):
                        act.wait_ge(gu_mm, 4 * t.n + 2 * f + 1)
                        wait(act, h_ok, 2 * t.n + f - 1)
                        act.activation(sg[:, f, :], ps[:, B_G + f, 0:FH], ACT.Silu).then_inc(sg_ok, 1)

                def hidden_out(t):
                    act.wait_ge(hT_mm, 2 * t.n + 1)
                    act.activation(hT[:, t.par, 0:4, :], ps[:, B_H, :].rearrange("p (c t) -> p c t", c=4),
                                   ACT.Copy).then_inc(hTa_ev, 1)

                def emit(t, n):
                    if n >= 1:
                        hidden_out(t - 1)
                    if n + 1 < TILES:
                        rows_out(t + 1)
                        silus(t + 1)

                steps(emit, act)

            @block.vector
            def _(dve):
                done = [0]

                def link(ins):
                    done[0] += 1
                    ins.then_inc(chain, 1)
                    dve.wait_ge(chain, done[0])

                dve.wait_ge(b_in, 16)
                dve.wait_ge(const, N_CONST)
                bc = [L, NB, E]
                link(dve.tensor_tensor(lg[:, :, :], LG[:, :, :], bs_bc[:, :].unsqueeze(1).to_broadcast(bc), ALU.add))
                for s in range(2):
                    link(dve.tensor_reduce(best[:, s, :], lg[:, :, :], AX_X, ALU.max))
                    link(dve.tensor_tensor(eq[:, :, :], lg[:, :, :], best[:, s, :].unsqueeze(2).to_broadcast(bc),
                                           ALU.is_equal))
                    link(dve.tensor_tensor(eq[:, :, :], eq[:, :, :], pref[:, :].unsqueeze(1).to_broadcast(bc), ALU.mult))
                    link(dve.tensor_reduce(top[:, :], eq[:, :, :], AX_X, ALU.max))
                    link(dve.tensor_tensor(oh[:, s, :, :], eq[:, :, :], top[:, :].unsqueeze(2).to_broadcast(bc),
                                           ALU.is_equal))
                    if s == 0:
                        link(dve.scalar_tensor_tensor(out=lg[:, :, :], in0=oh[:, 0, :, :], scalar=-3e38, in1=lg[:, :, :],
                                                      op0=ALU.mult, op1=ALU.add))
                dve.tensor_tensor(M[:, :, :], oh[:, 0, :, :], oh[:, 1, :, :], ALU.add).then_inc(M_ok, 1)
                dve.tensor_tensor(dm[:, :], best[:, 1, :], best[:, 0, :], ALU.subtract).then_inc(dm_ok, 1)
                dve.wait_ge(e2_ok, 1)
                link(dve.tensor_scalar(den[:, :], e2[:, :], 1.0, None, ALU.add))
                link(dve.reciprocal(w[:, 0, :], den[:, :]))
                link(dve.tensor_tensor(w[:, 1, :], e2[:, :], w[:, 0, :], ALU.mult))
                dve.wait_ge(cnt_mm, 1)
                HB = NB // 2
                link(dve.tensor_copy(run[0][:, HB:, :], ps[0:L, B_G + 1, 0:NB * E].rearrange("p (b e) -> p b e", b=NB)))
                a = 0
                for sh in (1, 2, 4, 8):
                    link(dve.tensor_tensor(run[1 - a][:, HB:, :], run[a][:, HB:, :],
                                           run[a][:, HB - sh:HB + NB - sh, :], ALU.add))
                    a = 1 - a
                total = run[a][:, HB + NB - 1, :]
                link(dve.tensor_tensor(more[:, :, :], total.unsqueeze(2).to_broadcast([L, E, JT]),
                                       step[:, :].unsqueeze(1).to_broadcast([L, E, JT]), ALU.is_gt))
                link(dve.tensor_reduce(off[0][:, E:], more[:, :, :], AX_X, ALU.add))
                o = 0
                for sh in (1, 2, 4):
                    link(dve.tensor_tensor(off[1 - o][:, E:], off[o][:, E:], off[o][:, E - sh:2 * E - sh], ALU.add))
                    o = 1 - o
                first_tile = off[o][:, E - 1:2 * E - 1]
                link(dve.tensor_scalar(off128[:, :], first_tile, float(P), None, ALU.mult))
                link(dve.tensor_tensor(pos[:, :, :], ps[0:L, B_G, 0:NB * E].rearrange("p (b e) -> p b e", b=NB),
                                       run[a][:, HB - 1:HB + NB - 1, :], ALU.add))
                link(dve.tensor_tensor(pos[:, :, :], pos[:, :, :], off128[:, :].unsqueeze(1).to_broadcast(bc), ALU.add))
                for s in range(2):
                    pr = dve.tensor_tensor(posc[:, s, :, :], pos[:, :, :], oh[:, s, :, :], ALU.mult)
                link(pr)
                link(dve.tensor_reduce(place[:, :, :], posc[:, :, :, :], AX_X, ALU.add))
                link(dve.tensor_copy(place_i[:, :, :], place[:, :, :]))
                pf = place_i[:, :, :].rearrange("p s b -> p (s b)")
                dve.tensor_scalar(hi_i[:, :], pf, P.bit_length() - 1, None, ALU.logical_shift_right)
                link(dve.tensor_scalar(lo_i[:, :], pf, P - 1, None, ALU.bitwise_and))
                dve.tensor_copy(hi[:, :], hi_i[:, :])
                link(dve.tensor_copy(lo[:, :], lo_i[:, :]))
                dve.tensor_tensor(ohl[:, :, :], lo[:, :].unsqueeze(2).to_broadcast([L, NBH, P]),
                                  iot[:, :].unsqueeze(1).to_broadcast([L, NBH, P]), ALU.is_equal)
                link(dve.tensor_tensor(ohh[:, :, :], hi[:, :].unsqueeze(2).to_broadcast([L, NBH, TILES]),
                                       iot[:, 0:TILES].unsqueeze(1).to_broadcast([L, NBH, TILES]), ALU.is_equal))
                for s in range(2):
                    ss = slice(s * NB, (s + 1) * NB)
                    dve.tensor_tensor(rh[:, ss, 0, :], ohh[:, ss, :],
                                      tok[:, :].unsqueeze(2).to_broadcast([L, NB, TILES]), ALU.mult)
                    r = dve.tensor_tensor(rh[:, ss, 1, :], ohh[:, ss, :],
                                          w[:, s, :].unsqueeze(2).to_broadcast([L, NB, TILES]), ALU.mult)
                r.then_inc(rh_ok, 1)
                link(dve.tensor_tensor(tex[:, :, :], iot[:, 0:TILES].unsqueeze(2).to_broadcast([L, TILES, E]),
                                       first_tile.unsqueeze(1).to_broadcast([L, TILES, E]), ALU.is_ge))
                link(dve.tensor_reduce(texf[:, :], tex[:, :, :], AX_X, ALU.add))
                dve.tensor_scalar(expert_of[:, :], texf[:, :], -1.0, None, ALU.add).then_inc(lists_ok, 1)
                dve.wait_ge(inv_mm, 1)
                dve.tensor_copy(wt[:, :], ps[:, B_Y, TILES:2 * TILES]).then_inc(chain, 1)
                done[0] += 1
                link(dve.tensor_copy(inv[:, :], ps[:, B_Y, 0:TILES]))
                dve.tensor_scalar(gat[:, :], inv[:, :], -1.0, 0.0, ALU.add, ALU.max).then_inc(lists_ok, 1)
                link(dve.tensor_scalar(pad[:, :], inv[:, :], 0.0, spare[:, 0:1], ALU.is_equal, ALU.mult))
                dve.scalar_tensor_tensor(out=sca[:, :], in0=inv[:, :], scalar=-1.0, in1=pad[:, :], op0=ALU.add,
                                         op1=ALU.add).then_inc(lists_ok, 1)

                def hidden(t):
                    for f in range(2):
                        dve.wait_ge(sg_ok, 2 * t.n + f + 1)
                        dve.wait_ge(gu_mm, 4 * t.n + 2 * f + 2)
                        wait(dve, hT_mm, 2 * t.n - 2)
                        dve.tensor_tensor(hh[:, t.par, f * FH:(f + 1) * FH], sg[:, f, :], ps[:, B_U + f, 0:FH],
                                          ALU.mult).then_inc(h_ok, 1)

                def hidden_out(t):
                    dve.wait_ge(hT_mm, 2 * t.n + 2)
                    dve.tensor_copy(hT[:, t.par, 4, :], ps[:, B_H + 1, 0:P])
                    dve.tensor_copy(hT[0:FR, t.par, 5, :], ps[0:FR, B_H + 1, P:2 * P]).then_inc(hTb_ev, 1)

                def weigh(t):
                    dve.wait_ge(y_mm, t.n + 1)
                    wait(dve, added, 16 * (t.n - 1))
                    dve.tensor_scalar(y[:, t.par, :], ps[:, B_Y, 0:D], wt[:, bass.ds(t.n, 1)], None,
                                      ALU.mult).then_inc(y_ok, 1)

                def emit(t, n):
                    if n >= 1:
                        hidden_out(t - 1)
                        weigh(t - 1)
                    if n + 1 < TILES:
                        hidden(t + 1)

                steps(emit, dve)

                def last_stats(q):
                    dve.wait_ge(acc_ins[q], 16)
                    for b in range(q * QB, (q + 1) * QB):
                        s = dve.bn_stats(stats[:, b, :], acc[:, b, :])
                    s.then_inc(st_ok, 1)
                    dve.wait_ge(st_ok, q + 1)
                    for b in range(q * QB, (q + 1) * QB):
                        m = dve.bn_aggr(mv[:, b, :], stats[:, b, :])
                    m.then_inc(mv_ok, 1)

                def last_norm(q):
                    dve.wait_ge(rstd_ok, q + 1)
                    for b in range(q * QB, (q + 1) * QB):
                        r = dve.tensor_scalar(acc[:, b, :], acc[:, b, :], mv[:, b, 0:1], rstd[:, b:b + 1],
                                              ALU.subtract, ALU.mult)
                    r.then_inc(res_ok, 1)

                last_stats(0)
                for q in range(4):
                    if q < 3:
                        last_stats(q + 1)
                    last_norm(q)


def load_experts(eng, WG, wg, WU, wu, landed):
    for e in range(E):
        eng.dma_start(WG[:, :, e, :], wg[e].rearrange("(k p) f -> p k f", p=P)).then_inc(landed, 16)
        eng.dma_start(WU[:, :, e, :], wu[e].rearrange("(k p) f -> p k f", p=P)).then_inc(landed, 16)


def decoder_layer(nc, x, xT, ctxT, sa_wqT, sa_wqkvT, sa_bqk, sa_bqkv, sa_wop, sa_w2T, sa_b2, wqT, wkT, wvT, woT, bqk, bv,
                  bo, ws, bs, wg, wu, wd, out):
    x1d = nc.dram_tensor("x1d", (NB, L, D), F32, kind="Internal").ap()
    x1Td = nc.dram_tensor("x1Td", (NB, P, KC, L), F32, kind="Internal").ap()
    x2d = nc.dram_tensor("x2d", (T, D), F32, kind="Internal").ap()
    accd = nc.dram_tensor("accd", (T, D), F32, kind="Internal").ap()
    with ExitStack() as ctx:
        ps = ctx.enter_context(nc.psum_tensor("ps", [P, 8, 512], F32))
        ident = ctx.enter_context(nc.sbuf_tensor("ident", [P, P], F32))
        LG = ctx.enter_context(nc.sbuf_tensor("LG", [L, NB, E], F32))
        WG = ctx.enter_context(nc.sbuf_tensor("WG", [P, KC, E, F], F32))
        WU = ctx.enter_context(nc.sbuf_tensor("WU", [P, KC, E, F], F32))
        self_attention(nc, ps, ident, x, xT, sa_wqT, sa_wqkvT, sa_bqk, sa_bqkv, sa_wop, sa_w2T, sa_b2, wg, wu, WG, WU,
                       load_experts, x1d, x1Td)
        cross_attention(nc, ps, ident, ctxT, wqT, wkT, wvT, woT, bqk, bv, bo, ws, x1d, x1Td, x2d, accd, LG)
        experts(nc, ps, ident, LG, bs, wd, WG, WU, x2d, accd, out)


def kernel(**inputs):
    import concourse.bacc as bacc
    from concourse.bass_utils import run_bass_kernel_spmd

    a = {k: np.asarray(v) for k, v in inputs.items()}

    def chunked(w):
        return w.reshape(-1, P, w.shape[-1]).transpose(1, 0, 2)

    def columns(v):
        return v.reshape(-1, P).T

    turned = np.arange(D).reshape(KC, P // DH, DH).transpose(0, 2, 1).reshape(-1)
    sa, xa = "L0_attn_", "L0_xattn_"
    lay = {
        "x": a["x"],
        "xT": chunked(a["x"].reshape(T, D).T),
        "ctxT": a["ctx_1024"].transpose(0, 2, 1).reshape(NB, KC, P, CTX).transpose(0, 2, 1, 3),
        "sa_wqT": chunked(a[sa + "Wq"].T),
        "sa_wqkvT": chunked(a[sa + "Wqkv"].T),
        "sa_bqk": columns(a[sa + "bqkv"][0:2 * D]),
        "sa_bqkv": a[sa + "bqkv"],
        "sa_wop": a[sa + "Wop"],
        "sa_w2T": a[sa + "W2"].T,
        "sa_b2": a[sa + "b2"],
        "wqT": chunked(a[xa + "wq"][turned].T),
        "wkT": chunked(a[xa + "wk"][turned].T),
        "wvT": chunked(a[xa + "wv"].T),
        "woT": chunked(a[xa + "wo"].T),
        "bqk": columns(np.concatenate([a[xa + "bq"][turned], a[xa + "bk"][turned]])),
        "bv": columns(a[xa + "bv"]),
        "bo": a[xa + "bo"],
        "ws": chunked(a["L0_ffn_Ws"]),
        "bs": a["L0_ffn_bs"],
        "wg": a["L0_ffn_Wg"],
        "wu": a["L0_ffn_Wu"],
        "wd": a["L0_ffn_Wd"],
    }
    nc = bacc.Bacc("TRN2", target_bir_lowering=False, num_devices=1)
    arrays, args = {}, {}
    for name, v in lay.items():
        v = np.ascontiguousarray(v)
        arrays["in_" + name] = v
        args[name] = nc.dram_tensor("in_" + name, v.shape, mybir.dt.from_np(v.dtype), kind="ExternalInput").ap()
    out = nc.dram_tensor("out", (NB, L, D), F32, kind="ExternalOutput").ap()
    decoder_layer(nc, **args, out=out)
    r = run_bass_kernel_spmd(nc, [arrays], core_ids=[0])
    return r.results[0]["out"]
```

```python
from contextlib import ExitStack

import numpy as np

import concourse.bass as bass
from concourse import mybir

F32 = mybir.dt.float32
BF16 = mybir.dt.bfloat16
U32 = mybir.dt.uint32
I32 = mybir.dt.int32
ALU = mybir.AluOpType
ACT = mybir.ActivationFunctionType
AX_X = mybir.AxisListType.X

P = 128
NB, L, D = 16, 100, 256
T = NB * L
KC = D // P
EPS = 1e-5

G, DG = 4, 64
WINDOWS = (32.0, 64.0, 128.0, 256.0)
NW = sum(w < L - 1 for w in WINDOWS)
PAIRS = NB // 2
BIG = 1e18

CTX = 361
H, DH = 16, 16
NCH = 3
CH = (CTX - 1) // NCH
CM = CH + 1
KQ = CTX + L
SLOTS = 6
PARTS = 3
SR = SLOTS * DH
VW = DH + 1
VC = 32
HG = P // VC
NG = H // HG
HH = H // 2
MR = PARTS * HH
MS = slice(SR, SR + MR)

E, F = 8, 688
TILES = (2 * T) // P + E - 1
FH = F // 2
FC = (F + P - 1) // P
FR = F - (FC - 1) * P


class Step:

    def __init__(self, i, c):
        self.i, self.c = i, c

    def __add__(self, k):
        return Step(self.i, self.c + k)

    def __sub__(self, k):
        return Step(self.i, self.c - k)

    @property
    def n(self):
        return 2 * self.i + self.c

    @property
    def half(self):
        return self.i + self.c // 2

    @property
    def par(self):
        return self.c % 2


def wait(eng, sem, count):
    if not isinstance(count, int) or count > 0:
        eng.wait_ge(sem, count)


def stand(eng, waits_met):
    eng.sem_inc(waits_met, 1)


def self_attention(nc, ps, ident, x, xT, wqT, wqkvT, bqk, bqkv, wop, w2T, b2, wg, wu, WG, WU, cross,
                   x1d, x1Td):
    with ExitStack() as ctx:
        def sb(name, shape, dt=F32):
            return ctx.enter_context(nc.sbuf_tensor(name, shape, dt))

        def sem(name):
            return ctx.enter_context(nc.semaphore(name))

        L2 = 2 * L
        wq_sb = sb("wq_sb", [P, KC, D])
        wqkv_sb = sb("wqkv_sb", [P, KC, 3 * D])
        wop_sb = sb("wop_sb", [64, D])
        w2_sb = sb("w2_sb", [64, 1])
        weff = sb("weff", [P, KC])
        bqk_sb = sb("bqk_sb", [P, 4])
        bv_bc = sb("bv_bc", [L, D])
        b2_bc = sb("b2_bc", [L, 1])
        negb2 = sb("negb2", [L, 1])
        xT_sb = sb("xT_sb", [P, KC, L2])
        x_sb = sb("x_sb", [L, 2, D])
        xb = sb("xb", [L, 2, D])
        qinT = sb("qinT", [P, KC, L2])
        rT = sb("rT", [P, KC, L2])
        qkT = sb("qkT", [P, 4, L2])
        va = sb("va", [L, 2, G, DG + 1])
        dist = sb("dist", [L, L])
        mask = sb("mask", [L, 2, 2, 2, L])
        edx = sb("edx", [L, 2])
        edx1 = sb("edx1", [L, 2])
        sig = sb("sig", [L, 2])
        thr = sb("thr", [L, 2, NW])
        s2 = sb("s2", [L, 2, G, L])
        mx = sb("mx", [L, 2, G])
        pr = sb("pr", [L, 2, G * L])
        prT = sb("prT", [L, 2, G * L])
        rc = sb("rc", [L, 2, G, 1])
        o = sb("o", [L, 2, D])
        xr = sb("xr", [L, 2, D])
        stats = sb("stats", [L, 2, 6])
        mv = sb("mv", [L, 2, 2])
        ve = sb("ve", [L, 2])
        rstd = sb("rstd", [L, 2])
        mhalf = sb("mhalf", [L, 2])
        x1 = sb("x1", [L, 2, D])
        x1T = sb("x1T", [P, 2, KC, L])

        wq_in, wqkv_in, w_in = sem("wq_in"), sem("wqkv_in"), sem("w_in")
        xT_in, x_in = sem("xT_in"), sem("x_in")
        experts_in, cross_in = sem("experts_in"), sem("cross_in")
        own_step, own_ok, own_rows_ok, cva_set = sem("own_step"), sem("own_ok"), sem("own_rows_ok"), sem("cva_set")
        id_set, consts = sem("id_set"), sem("consts")
        weff_mm, weff_ev = sem("weff_mm"), sem("weff_ev")
        xb_ok = sem("xb_ok")
        q_mm, q_ev, r_ok = sem("q_mm"), sem("q_ev"), sem("r_ok")
        qk_mm, qk_ev = sem("qk_mm"), sem("qk_ev")
        v_mm, v_ev = sem("v_mm"), sem("v_ev")
        dx_mm, dx_ev, thr_step, mask_ok = sem("dx_mm"), sem("dx_ev"), sem("thr_step"), sem("mask_ok")
        s_mm, s2_step, s2_ok, p_ok = sem("s_mm"), sem("s2_step"), sem("s2_ok"), sem("p_ok")
        pT_mm, pT_ev, pv_mm, rc_ok, pv_rd = sem("pT_mm"), sem("pT_ev"), sem("pv_mm"), sem("rc_ok"), sem("pv_rd")
        xr_ok, st_ok, mv_ok, ve_ok, rstd_ok, x1_ok = (sem("xr_ok"), sem("st_ok"), sem("mv_ok"), sem("ve_ok"),
                                                      sem("rstd_ok"), sem("x1_ok"))
        xT_mm, xT_ev = sem("xT_mm"), sem("xT_ev")
        x1_out, x1T_out = sem("x1_out"), sem("x1T_out")
        dve_stands, pool_stands = sem("dve_stands"), sem("pool_stands")

        B_QIN, B_QK, B_V, B_S, B_PV = 0, 1, 3, 4, 6
        N_W = 5 * 16

        with nc.Block() as block:

            @block.sync
            def _(sp):
                def load_xT(g):
                    sp.dma_start(xT_sb[:, :, :], xT[:, :, bass.ds(g * L2, L2)]).then_inc(xT_in, 16)

                def load_x(g):
                    sp.dma_start(x_sb[:, :, :], x[bass.ds(2 * g, 2), :, :].rearrange("u l d -> l u d")).then_inc(x_in, 16)

                sp.dma_start(wq_sb[:, :, :], wqT).then_inc(wq_in, 16)
                load_xT(0)
                sp.dma_start(wqkv_sb[:, :, :], wqkvT).then_inc(wqkv_in, 16)
                sp.dma_start(bqk_sb[:, :], bqk).then_inc(w_in, 16)
                sp.dma_start(wop_sb[:, :], wop).then_inc(w_in, 16)
                sp.dma_start(w2_sb[:, :], w2T).then_inc(w_in, 16)
                sp.dma_start(b2_bc[:, :], b2.partition_broadcast(L)).then_inc(w_in, 16)
                sp.dma_start(bv_bc[:, :], bqkv[2 * D:3 * D].partition_broadcast(L)).then_inc(w_in, 16)
                load_x(0)

                def store(g):
                    sp.wait_ge(x1_ok, g + 1)
                    sp.dma_start(x1d[bass.ds(2 * g, 2), :, :].rearrange("u l d -> l u d"), x1[:, :, :]).then_inc(x1_out, 16)

                def store_T(g):
                    sp.wait_ge(xT_ev, g + 1)
                    sp.dma_start(x1Td[bass.ds(2 * g, 2), :, :, :].rearrange("u p k l -> p u k l"),
                                 x1T[:, :, :, :]).then_inc(x1T_out, 16)

                def next_xT(g):
                    sp.wait_ge(q_mm, g + 1)
                    load_xT(g + 1)

                def next_x(g):
                    sp.wait_ge(xb_ok, g + 1)
                    load_x(g + 1)

                next_xT(0)
                next_x(0)
                cross.load(sp, cross_in)
                for g in (1, 2):
                    next_xT(g)
                    next_x(g)
                    store(g - 1)
                with sp.Fori(3, PAIRS - 1) as g:
                    next_xT(g)
                    store_T(g - 3)
                    next_x(g)
                    store(g - 1)
                store_T(PAIRS - 4)
                store(PAIRS - 2)
                store_T(PAIRS - 3)
                store(PAIRS - 1)
                store_T(PAIRS - 2)
                store_T(PAIRS - 1)
                sp.wait_ge(x1_out, 16 * PAIRS)
                sp.wait_ge(x1T_out, 16 * PAIRS)
                sp.wait_ge(cross_in, 16 * cross.LOADS)

            @block.gpsimd
            def _(pool):
                mask4 = mask[:, :, :, :, :].rearrange("p a u b l -> p a (u b) l")
                cross.find_own(pool, own_step, own_ok)
                pool.wait_ge(own_ok, 1)
                pool.memset(ident[:, :], 0.0).then_inc(id_set, 1)
                pool.wait_ge(id_set, 1)
                pool.affine_select(out=ident[:, :], in_=ident[:, :], compare_op=ALU.not_equal, fill=1.0, base=0,
                                   pattern=[[-1, P]], channel_multiplier=1).then_inc(consts, 1)
                pool.iota(dist[:, :], pattern=[[1, L]], base=0, channel_multiplier=-1,
                          allow_small_or_imprecise_dtypes=True).then_inc(id_set, 1)
                pool.memset(mask4, 0.0).then_inc(id_set, 1)
                pool.memset(va[:, :, :, DG:DG + 1], 1.0).then_inc(consts, 1)
                pool.memset(mhalf[:, :], -0.5).then_inc(consts, 1)
                pool.wait_ge(id_set, 3)
                pool.affine_select(out=dist[:, :], in_=dist[:, :], compare_op=ALU.is_ge, fill=BIG, base=0,
                                   pattern=[[1, L]], channel_multiplier=-1).then_inc(consts, 1)
                pool.affine_select(out=mask4, in_=mask4, compare_op=ALU.is_ge, fill=-BIG, base=0,
                                   pattern=[[0, 2], [0, 4], [1, L]], channel_multiplier=-1).then_inc(consts, 1)
                pool.wait_ge(w_in, N_W)
                pool.wait_ge(consts, 5)
                for u in range(2):
                    pool.memset(cross.va[u][:, :, :, DH:VC], 1.0).then_inc(cva_set, 1)
                pool.wait_ge(cva_set, 2)
                pool.tensor_scalar_mul(negb2[:, :], b2_bc[:, :], -1.0).then_inc(consts, 1)

                def add_bias(g):
                    pool.wait_ge(x_in, 16 * (g + 1))
                    wait(pool, xr_ok, 2 * g)
                    pool.tensor_tensor(xb[:, :, :], x_sb[:, :, :],
                                       bv_bc[:, :].unsqueeze(1).to_broadcast([L, 2, D]), ALU.add).then_inc(xb_ok, 1)

                def rstd_of(g):
                    pool.wait_ge(mv_ok, 2 * g + 2)
                    stand(pool, pool_stands)
                    pool.tensor_scalar(ve[:, :], mv[:, :, 1], EPS, None, ALU.add).then_inc(ve_ok, 1)
                    pool.wait_ge(ve_ok, g + 1)
                    pool.tensor_tensor(rstd[:, :], ve[:, :], mhalf[:, :], ALU.pow).then_inc(rstd_ok, 1)

                add_bias(0)
                with pool.Fori(1, PAIRS) as g:
                    add_bias(g)
                    rstd_of(g - 1)
                rstd_of(PAIRS - 1)

            @block.tensor
            def _(pe):
                pe.wait_ge(wq_in, 16)

                def q_in(g):
                    pe.wait_ge(xT_in, 16 * (g + 1))
                    wait(pe, dx_ev, g)
                    for m in range(KC):
                        for k in range(KC):
                            mm = pe.matmul(ps[:, B_QIN, m * L2:(m + 1) * L2], wq_sb[:, k, m * P:(m + 1) * P],
                                           xT_sb[:, k, :], start=(k == 0), stop=(k == KC - 1))
                    mm.then_inc(q_mm, 1)

                def qk(g, half):
                    if half == 0:
                        pe.wait_ge(q_ev, g + 1)
                    wait(pe, qk_ev, 2 * g)
                    for m in range(2):
                        c = 2 * half + m
                        for k in range(KC):
                            mm = pe.matmul(ps[:, B_QK + half, m * L2:(m + 1) * L2], wqkv_sb[:, k, c * P:(c + 1) * P],
                                           qinT[:, k, :], start=(k == 0), stop=(k == KC - 1))
                    mm.then_inc(qk_mm, 1)

                def values(g):
                    wait(pe, xT_ev, g - 2)
                    for u in range(2):
                        for k in range(KC):
                            mm = pe.matmul(ps[0:L, B_V, u * D:(u + 1) * D], qinT[:, k, u * L:(u + 1) * L],
                                           wqkv_sb[:, k, 2 * D:3 * D], start=(k == 0), stop=(k == KC - 1))
                    mm.then_inc(v_mm, 1)

                def learned_window(g):
                    pe.wait_ge(r_ok, g + 1)
                    for u in range(2):
                        for k in range(KC):
                            mm = pe.matmul(ps[0:L, B_QIN, 2 * L2 + u:2 * L2 + u + 1], rT[:, k, u * L:(u + 1) * L],
                                           weff[:, k:k + 1], start=(k == 0), stop=(k == KC - 1))
                    mm.then_inc(dx_mm, 1)

                def scores(g, first):
                    pe.wait_ge(qk_ev, 2 * g + 2)
                    if not first:
                        pe.wait_ge(pT_ev, 2 * g)
                    for c in range(4):
                        u, hh = c // 2, c % 2
                        for hp in range(2):
                            r = DG * hp
                            mm = pe.matmul(ps[0:L, B_S + hp, c * L:(c + 1) * L], qkT[r:r + DG, hh, u * L:(u + 1) * L],
                                           qkT[r:r + DG, 2 + hh, u * L:(u + 1) * L], start=True, stop=True)
                            if c == 3:
                                mm.then_inc(s_mm, 1)

                def turn_probs(g):
                    for hp in range(2):
                        pe.wait_ge(p_ok, 2 * g + hp + 1)
                        for c in range(4):
                            mm = pe.transpose(ps[0:L, B_S + hp, c * L:(c + 1) * L], pr[:, hp, c * L:(c + 1) * L],
                                              ident[0:L, 0:L])
                        mm.then_inc(pT_mm, 1)

                def weigh_values(g):
                    pe.wait_ge(pT_ev, 2 * g + 2)
                    pe.wait_ge(v_ev, g + 1)
                    wait(pe, pv_rd, 2 * g)
                    for u in range(2):
                        for h in range(G):
                            mm = pe.matmul(ps[0:L, B_PV + u, h * (DG + 1):(h + 1) * (DG + 1)],
                                           prT[:, h % 2, (2 * u + h // 2) * L:(2 * u + h // 2 + 1) * L],
                                           va[:, u, h, :], start=True, stop=True)
                        mm.then_inc(pv_mm, 1)

                def turn_x1(g):
                    pe.wait_ge(x1_ok, g + 1)
                    pe.wait_ge(v_ev, min(g + 3, PAIRS) if isinstance(g, int) else g + 3)
                    for u in range(2):
                        for k in range(KC):
                            c = u * KC + k
                            mm = pe.transpose(ps[:, B_V, c * L:(c + 1) * L], x1[:, u, k * P:(k + 1) * P],
                                              ident[0:L, 0:L])
                    mm.then_inc(xT_mm, 1)

                q_in(0)
                pe.wait_ge(wqkv_in, 16)
                qk(0, 0)
                qk(0, 1)
                values(0)
                pe.wait_ge(w_in, N_W)
                for k in range(KC):
                    mm = pe.matmul(ps[:, B_PV, k:k + 1], wop_sb[:, k * P:(k + 1) * P], w2_sb[:, :], start=True, stop=True)
                mm.then_inc(weff_mm, 1)
                pe.wait_ge(weff_ev, 1)
                learned_window(0)
                scores(0, True)
                pe.wait_ge(consts, 6)

                def step(g, first=False):
                    q_in(g)
                    qk(g, 0)
                    qk(g, 1)
                    values(g)
                    turn_probs(g - 1)
                    learned_window(g)
                    weigh_values(g - 1)
                    scores(g, False)
                    if not first:
                        turn_x1(g - 2)

                step(1, first=True)
                step(2)
                with pe.Fori(3, PAIRS) as g:
                    step(g)
                turn_probs(PAIRS - 1)
                weigh_values(PAIRS - 1)
                pe.wait_ge(xT_ev, PAIRS - 2)
                turn_x1(PAIRS - 2)
                pe.wait_ge(xT_ev, PAIRS - 1)
                turn_x1(PAIRS - 1)

            @block.scalar
            def _(act):
                def load_expert(e):
                    for W, w in ((WG, wg), (WU, wu)):
                        act.dma_start(W[:, :, bass.ds(e, 1), :],
                                      w[bass.ds(e, 1), :, :].rearrange("e (k p) f -> p k e f", p=P)).then_inc(experts_in, 16)

                def projections(g):
                    act.wait_ge(q_mm, g + 1)
                    act.activation(qinT[:, :, :], ps[:, B_QIN, 0:2 * L2].rearrange("p (m t) -> p m t", m=KC),
                                   ACT.Copy).then_inc(q_ev, 1)

                def probs_out(g, u):
                    act.wait_ge(pT_mm, 2 * g + u + 1)
                    act.activation(prT[:, u, :], ps[0:L, B_S + u, 0:G * L], ACT.Copy).then_inc(pT_ev, 1)

                def qk_out(g, half):
                    act.wait_ge(qk_mm, 2 * g + half + 1)
                    for m in range(2):
                        c = 2 * half + m
                        cp = act.activation(qkT[:, c, :], ps[:, B_QK + half, m * L2:(m + 1) * L2], ACT.Identity,
                                            bias=bqk_sb[:, c:c + 1])
                    cp.then_inc(qk_ev, 1)

                def v_out(g):
                    act.wait_ge(v_mm, g + 1)
                    wait(act, pv_mm, 2 * g)
                    act.activation(va[:, :, :, 0:DG], ps[0:L, B_V, :].rearrange("p (u h d) -> p u h d", u=2, h=G),
                                   ACT.Copy).then_inc(v_ev, 1)

                def window_out(g):
                    act.wait_ge(dx_mm, g + 1)
                    wait(act, thr_step, 2 * g)
                    act.activation(edx[:, :], ps[0:L, B_QIN, 2 * L2:2 * L2 + 2], ACT.Exp, bias=negb2[:, 0:1],
                                   scale=-1.0).then_inc(dx_ev, 1)

                def exps(g, u):
                    act.wait_ge(s2_ok, 2 * g + u + 1)
                    act.activation(pr[:, u, :], s2[:, u, :, :].rearrange("p h l -> p (h l)"), ACT.Exp).then_inc(p_ok, 1)

                def x1T_copy(g):
                    act.wait_ge(xT_mm, g + 1)
                    wait(act, x1T_out, 16 * g)
                    act.activation(x1T[:, :, :, :],
                                   ps[:, B_V, 0:2 * KC * L].rearrange("p (u k l) -> p u k l", u=2, k=KC),
                                   ACT.Copy).then_inc(xT_ev, 1)

                def weff_out():
                    act.wait_ge(weff_mm, 1)
                    act.activation(weff[:, :], ps[:, B_PV, 0:KC], ACT.Copy).then_inc(weff_ev, 1)

                def step(g, first=False):
                    projections(g)
                    for half in range(2):
                        exps(g - 1, half)
                        qk_out(g, half)
                    load_expert(g - 1)
                    probs_out(g - 1, 0)
                    probs_out(g - 1, 1)
                    window_out(g)
                    v_out(g)
                    if not first:
                        x1T_copy(g - 2)

                act.wait_ge(own_ok, 1)
                rows, source = cross.own_rows(1)
                act.activation(rows, source, ACT.Copy).then_inc(own_rows_ok, 1)
                projections(0)
                act.wait_ge(w_in, N_W)
                act.wait_ge(consts, 6)
                qk_out(0, 0)
                qk_out(0, 1)
                v_out(0)
                weff_out()
                window_out(0)
                step(1, first=True)
                step(2)
                with act.Fori(3, PAIRS) as g:
                    step(g)
                load_expert(PAIRS - 1)
                for half in range(2):
                    exps(PAIRS - 1, half)
                    probs_out(PAIRS - 1, half)
                x1T_copy(PAIRS - 2)
                x1T_copy(PAIRS - 1)
                act.wait_ge(experts_in, 16 * 2 * E)
                act.wait_ge(own_rows_ok, 2)

            @block.vector
            def _(dve):
                dve.wait_ge(own_ok, 1)
                rows, source = cross.own_rows(0)
                dve.tensor_copy(rows, source).then_inc(own_rows_ok, 1)
                dve.wait_ge(consts, 6)

                def relu(g):
                    dve.wait_ge(q_ev, g + 1)
                    wait(dve, dx_mm, g)
                    dve.tensor_scalar(rT[:, :, :], qinT[:, :, :], 0.0, None, ALU.max).then_inc(r_ok, 1)

                def normalise(g):
                    for u in range(2):
                        pv = ps[0:L, B_PV + u, 0:G * (DG + 1)].rearrange("p (h w) -> p h w", h=G)
                        dve.wait_ge(pv_mm, 2 * g + u + 1)
                        dve.reciprocal(rc[:, u, :, :], pv[:, :, DG:DG + 1]).then_inc(rc_ok, 1)
                        dve.wait_ge(rc_ok, 2 * g + u + 1)
                        dve.tensor_tensor(o[:, u, :].rearrange("p (h d) -> p h d", h=G), pv[:, :, 0:DG],
                                          rc[:, u, :, :].to_broadcast([L, G, DG]), ALU.mult).then_inc(pv_rd, 1)
                        dve.wait_ge(pv_rd, 2 * g + u + 1)
                        dve.wait_ge(xb_ok, g + 1)
                        dve.tensor_tensor(xr[:, u, :], o[:, u, :], xb[:, u, :], ALU.add).then_inc(xr_ok, 1)
                        dve.wait_ge(xr_ok, 2 * g + u + 1)
                        dve.bn_stats(stats[:, u, :], xr[:, u, :]).then_inc(st_ok, 1)
                        dve.wait_ge(st_ok, 2 * g + u + 1)
                        if u == 0:
                            wait(dve, rstd_ok, g)
                        stand(dve, dve_stands)
                        dve.bn_aggr(mv[:, u, :], stats[:, u, :]).then_inc(mv_ok, 1)

                def apply(g):
                    dve.wait_ge(rstd_ok, g + 1)
                    wait(dve, x1_out, 16 * g)
                    wait(dve, xT_mm, g)
                    for u in range(2):
                        ap = dve.tensor_scalar(x1[:, u, :], xr[:, u, :], mv[:, u, 0:1], rstd[:, u:u + 1],
                                               ALU.subtract, ALU.mult)
                    ap.then_inc(x1_ok, 1)

                def masks(g):
                    dve.wait_ge(dx_ev, g + 1)
                    dve.tensor_scalar(edx1[:, :], edx[:, :], 1.0, None, ALU.add).then_inc(thr_step, 1)
                    dve.wait_ge(thr_step, 2 * g + 1)
                    dve.reciprocal(sig[:, :], edx1[:, :]).then_inc(thr_step, 1)
                    dve.wait_ge(thr_step, 2 * g + 2)
                    for w in range(NW):
                        th = dve.tensor_scalar(thr[:, :, w], sig[:, :], float(L), WINDOWS[w], ALU.mult, ALU.add)
                    th.then_inc(mask_ok, 1)
                    dve.wait_ge(mask_ok, 2 * g + 1)
                    for u in range(2):
                        for w in range(NW):
                            mk = dve.tensor_scalar(mask[:, w, u, 0, :], dist[:, :], thr[:, u, w:w + 1], -BIG,
                                                   ALU.is_gt, ALU.mult)
                    mk.then_inc(mask_ok, 1)

                def softmax_in(g):
                    for hp in range(2):
                        n = 2 * g + hp
                        if hp == 0:
                            dve.wait_ge(mask_ok, 2 * g + 2)
                        dve.wait_ge(s_mm, n + 1)
                        wait(dve, p_ok, n - 1)
                        dve.scalar_tensor_tensor(out=s2[:, hp, :, :],
                                                 in0=ps[0:L, B_S + hp, 0:G * L].rearrange("p (h l) -> p h l", h=G),
                                                 scalar=2.0 * float(np.float32(1.0 / np.sqrt(L))),
                                                 in1=mask[:, hp, :, :, :].rearrange("p u b l -> p (u b) l"), op0=ALU.mult, op1=ALU.add).then_inc(s2_step, 1)
                        dve.wait_ge(s2_step, 2 * n + 1)
                        dve.tensor_reduce(mx[:, hp, :], s2[:, hp, :, :], AX_X, ALU.max).then_inc(s2_step, 1)
                        dve.wait_ge(s2_step, 2 * n + 2)
                        dve.tensor_tensor(s2[:, hp, :, :], s2[:, hp, :, :],
                                          mx[:, hp, :].unsqueeze(2).to_broadcast([L, G, L]),
                                          ALU.subtract).then_inc(s2_ok, 1)

                relu(0)
                masks(0)
                softmax_in(0)

                def step(g):
                    relu(g)
                    masks(g)
                    normalise(g - 1)
                    softmax_in(g)
                    apply(g - 1)

                step(1)
                with dve.Fori(2, PAIRS) as g:
                    step(g)
                normalise(PAIRS - 1)
                apply(PAIRS - 1)


class CrossOperands:

    def __init__(self, nc, ctx, ctxT, wqT, wkT, wvT, woT, bqk, bv, bo, ws):
        def sb(name, shape):
            return ctx.enter_context(nc.sbuf_tensor(name, shape, F32))

        self.wq = sb("cwq_sb", [P, KC, D])
        self.wk = sb("cwk_sb", [P, KC, D])
        self.wv = sb("cwv_sb", [P, KC, D])
        self.wo = sb("cwo_sb", [P, KC, D])
        self.ws = sb("ws_sb", [P, KC, E])
        self.bqk = sb("cbqk_sb", [P, 2 * KC])
        self.bv = sb("cbv_sb", [P, KC])
        self.bo = sb("bo_bc", [L, D])
        self.cx = [sb(f"cx{u}", [P, KC, CTX]) for u in range(2)]
        self.st = [ctx.enter_context(nc.sbuf_tensor(f"st{u}", [SR + MR, H, KQ], BF16)) for u in range(2)]
        self.own = sb("own", [SR + MR, H])
        self.va = [sb(f"cva{u}", [CM, NCH, H, VC]) for u in range(2)]
        self.sources = ((self.wk, wkT), (self.wq, wqT), (self.wv, wvT), (self.wo, woT), (self.ws, ws),
                        (self.bqk, bqk), (self.bv, bv), (self.bo, bo.partition_broadcast(L)),
                        (self.cx[0], ctxT[0]), (self.cx[1], ctxT[1]))
        self.LOADS = len(self.sources)

    def find_own(self, pool, step, found):
        pool.memset(self.own[MS, :], 0.0).then_inc(step, 1)
        o = self.own[MS, :].rearrange("p (u h) -> p u h", u=2)
        for r in range(PARTS):
            pool.wait_ge(step, r + 1)
            sel = pool.affine_select(out=o, in_=o, compare_op=ALU.not_equal, fill=1.0, base=-r * HH,
                                     pattern=[[0, 2], [-1, HH]], channel_multiplier=1)
            sel.then_inc(step if r < PARTS - 1 else found, 1)

    def own_rows(self, u):
        return self.st[u][MS, :, 0:CTX], self.own[MS, :].unsqueeze(2).to_broadcast([MR, H, CTX])

    def load(self, eng, landed):
        for tile, source in self.sources:
            whole = tile[:, :, :] if len(tile.shape) == 3 else tile[:, :]
            eng.dma_start(whole, source).then_inc(landed, 16)


def cross_attention(nc, ps, ident, ctxT, cross, x1d, x1Td, x2d, accd, LG):
    with ExitStack() as ctx:
        def sb(name, shape, dt=F32):
            return ctx.enter_context(nc.sbuf_tensor(name, shape, dt))

        def sem(name):
            return ctx.enter_context(nc.semaphore(name))

        wq_sb, wk_sb, wv_sb, wo_sb, ws_sb = cross.wq, cross.wk, cross.wv, cross.wo, cross.ws
        bqk_sb, bv_sb, bo_bc, cx, st, va = cross.bqk, cross.bv, cross.bo, cross.cx, cross.st, cross.va
        bq4 = sb("bq4", [P, KC])
        bvr = sb("bvr", [P, KC, L])
        cbc = sb("cbc", [L, D])
        negid = sb("negid", [L, L], BF16)
        mhalf = sb("mhalf2", [L, 1])
        x1T_sb = sb("x1T_sb", [P, KC, L])
        x1_sb = sb("x1_sb", [L, D])
        x1b = sb("x1b", [L, D])
        kf = sb("kf", [P, KC, KQ])
        rf = sb("rf", [P, KC, KQ])
        parts = [sb(f"parts{u}", [P, KC, SLOTS, KQ], BF16) for u in range(2)]
        pr = sb("cpr", [CM, 2 * HG, NCH * L])
        oT = sb("oT", [P, NG, L])
        mx = sb("cmx", [L, 2, HH])
        mxr = sb("mxr", [L, 2, HH])
        mxp = sb("mxp", [L, 2, SR + MR], BF16)
        rc = sb("crc", [L, H, 1])
        at = sb("at", [L, D])
        atT = sb("atT", [P, KC, L])
        xr = sb("cxr", [L, D])
        stats = sb("cstats", [L, 6])
        mv = sb("cmv", [L, 2])
        ve = sb("cve", [L, 1])
        rstd = sb("crstd", [L, 1])
        x2 = sb("x2", [L, D])
        x2T = sb("x2T", [P, KC, L])

        names = ("ones_set c_step c_mm c_ok kf_set x1T_in x1_in k_mm q_mm k_ev q_ev k1_ok r_ok k2_ok k3_ok "
                 "v_mm v_ev s_mm max_ok t_mm exp_ok pv_mm oT_ev o_mm rc_ok at_ok aT_mm aT_ev wo_mm x1b_ok wo_rd st_ok mv_ok "
                 "ve_ok rstd_ok x2_ok x2_out x2T_mm x2T_ev lg_mm lg_ev").split()
        (ones_set, c_step, c_mm, c_ok, kf_set, x1T_in, x1_in, k_mm, q_mm, k_ev, q_ev, k1_ok, r_ok, k2_ok,
         k3_ok, v_mm, v_ev, s_mm, max_ok, t_mm, exp_ok, pv_mm, oT_ev, o_mm, rc_ok, at_ok, aT_mm, aT_ev, wo_mm, x1b_ok,
         wo_rd, st_ok, mv_ok, ve_ok, rstd_ok, x2_ok, x2_out, x2T_mm, x2T_ev, lg_mm, lg_ev) = [sem("c_" + n) for n in names]
        dve_stands, pool_stands, sp_stands = sem("c_dve_stands"), sem("c_pool_stands"), sem("c_sp_stands")
        cx_in = [sem(f"cx_in{u}") for u in range(2)]
        kq_in = [sem(f"kq_in{u}") for u in range(2)]
        mxp_step = [sem(f"mxp_step{u}") for u in range(2)]
        mxp_ok = [sem(f"mxp_ok{u}") for u in range(2)]
        mT_mm = [sem(f"mT_mm{u}") for u in range(2)]
        mT_ev = [sem(f"mT_ev{u}") for u in range(2)]

        B_S, B_T, B_O, M0, M1, M2 = 0, 2, 4, 5, 6, 7

        def steps(emit, eng):
            def one(b, lo):
                emit(b, 0 <= lo + 2 < NB, 0 <= lo + 1 < NB, 0 <= lo < NB, 0 <= lo - 1 < NB, lo + 3 < NB)

            for b in (-2, -1, 0, 1):
                one(Step(0, b), b)
            with eng.Fori(0, (NB - 6) // 2) as i:
                for c in (2, 3):
                    one(Step(i, c), c)
            for b in range(NB - 4, NB + 1):
                one(Step(0, b), b)

        with nc.Block() as block:

            @block.sync
            def _(sp):
                def load_ctx(b):
                    sp.dma_start(cx[b.par][:, :, :], ctxT[bass.ds(b.n, 1), :, :, :].rearrange("o p k c -> p (o k) c"))\
                        .then_inc(cx_in[b.par], 16)

                def load_x1T(b):
                    sp.dma_start(x1T_sb[:, :, :], x1Td[bass.ds(b.n, 1), :, :, :].rearrange("o p k l -> p (o k) l"))\
                        .then_inc(x1T_in, 16)

                def load_x1(b):
                    sp.dma_start(x1_sb[:, :], x1d[bass.ds(b.n, 1), :, :].rearrange("o l d -> (o l) d")).then_inc(x1_in, 16)

                load_x1T(Step(0, 0))

                def stack(b, half):
                    hs = slice(half * HH, (half + 1) * HH)
                    src = parts[b.par]
                    wait(sp, kq_in[half], 16 * SLOTS * b.n)
                    for s in range(SLOTS):
                        sp.dma_start(st[b.par][s * DH:(s + 1) * DH, hs, :], src[:, half, s, :]).then_inc(kq_in[half], 16)

                def emit(b, kq, s, t, tail, more):
                    if kq and more:
                        sp.wait_ge(q_mm, b.n + 3)
                        load_x1T(b + 3)
                    if kq:
                        sp.wait_ge(k3_ok, 2 * b.n + 5)
                        stand(sp, sp_stands)
                        wait(sp, t_mm, H * b.n + HH)
                        stand(sp, sp_stands)
                        stack(b + 2, 0)
                    if s and more:
                        sp.wait_ge(v_mm, 2 * b.n + 4)
                        stand(sp, sp_stands)
                        load_ctx(b + 3)
                    if t:
                        wait(sp, x1b_ok, b.n)
                        load_x1(b)
                    if tail:
                        sp.wait_ge(x2_ok, b.n)
                        for dst in (x2d, accd):
                            sp.dma_start(dst[bass.ds((b.n - 1) * L, L), :], x2[:, :]).then_inc(x2_out, 16)
                    if kq:
                        sp.wait_ge(k3_ok, 2 * b.n + 6)
                        stand(sp, sp_stands)
                        wait(sp, t_mm, H * b.n + H)
                        stand(sp, sp_stands)
                        stack(b + 2, 1)

                steps(emit, sp)
                sp.wait_ge(x2_out, 32 * NB)

            @block.gpsimd
            def _(pool):
                pool.memset(mhalf[:, :], -0.5).then_inc(ones_set, 1)
                pool.memset(mxp[:, :, 0:SR], 0.0).then_inc(ones_set, 1)
                pool.tensor_scalar_mul(negid[:, :], ident[0:L, 0:L], -1.0).then_inc(ones_set, 1)

                def part(half, r):
                    return mxp[:, half, SR + r * HH:SR + (r + 1) * HH]

                def split_maximum(b, half):
                    pool.wait_ge(max_ok, H * b.n + HH * (half + 1))
                    wait(pool, mT_mm[half], b.n)
                    stand(pool, pool_stands)
                    pool.tensor_copy(part(half, 0), mx[:, half, :]).then_inc(mxp_step[half], 1)
                    pool.wait_ge(mxp_step[half], 3 * b.n + 1)
                    pool.tensor_tensor(mxr[:, half, :], mx[:, half, :], part(half, 0),
                                       ALU.subtract).then_inc(mxp_step[half], 1)
                    pool.wait_ge(mxp_step[half], 3 * b.n + 2)
                    stand(pool, pool_stands)
                    pool.tensor_copy(part(half, 1), mxr[:, half, :]).then_inc(mxp_step[half], 1)
                    pool.wait_ge(mxp_step[half], 3 * b.n + 3)
                    pool.tensor_tensor(part(half, 2), mxr[:, half, :], part(half, 1),
                                       ALU.subtract).then_inc(mxp_ok[half], 1)

                def emit(b, kq, s, t, tail, more):
                    if t:
                        split_maximum(b, 1)
                    if tail:
                        pool.wait_ge(x1_in, 16 * b.n)
                        wait(pool, wo_rd, b.n - 1)
                        pool.wait_ge(c_ok, 1)
                        pool.tensor_tensor(x1b[:, :], x1_sb[:, :], cbc[:, :], ALU.add).then_inc(x1b_ok, 1)
                    if s:
                        split_maximum(b + 1, 0)
                    if tail:
                        pool.wait_ge(mv_ok, b.n)
                        stand(pool, pool_stands)
                        pool.tensor_scalar(ve[:, :], mv[:, 1:2], EPS, None, ALU.add).then_inc(ve_ok, 1)
                        pool.wait_ge(ve_ok, b.n)
                        pool.tensor_tensor(rstd[:, :], ve[:, :], mhalf[:, :], ALU.pow).then_inc(rstd_ok, 1)

                steps(emit, pool)

            @block.tensor
            def _(pe):
                pe.wait_ge(ones_set, 3)
                pe.wait_ge(c_step, 2)
                for k in range(KC):
                    mm = pe.matmul(ps[0:L, B_O, 0:D], bvr[:, k, :], wo_sb[:, k, :], start=(k == 0), stop=(k == KC - 1))
                mm.then_inc(c_mm, 1)
                pe.wait_ge(c_ok, 1)

                def query_scores(b, h):
                    half, hh = divmod(h, HH)
                    if hh == 0:
                        pe.wait_ge(kq_in[half], 16 * SLOTS * (b.n + 1))
                    wait(pe, max_ok, H * b.n + h - 1)
                    pe.matmul(ps[0:L, B_S + h % 2, 0:CTX], st[b.par][0:SR, h, CTX:KQ], st[b.par][0:SR, h, 0:CTX],
                              start=True, stop=True).then_inc(s_mm, 1)

                def key_scores(b, h):
                    half, hh = divmod(h, HH)
                    if hh == 0:
                        pe.wait_ge(mT_ev[half], b.n + 1)
                    wait(pe, exp_ok, H * b.n + h - 1)
                    for c in range(NCH):
                        mm = pe.matmul(ps[0:CM, B_T + h % 2, c * L:(c + 1) * L],
                                       st[b.par][:, h, c * CH:c * CH + CM], st[b.par][:, h, CTX:KQ],
                                       start=True, stop=True)
                    mm.then_inc(t_mm, 1)

                def weigh_values(b, g):
                    pe.wait_ge(exp_ok, H * b.n + HG * (g + 1))
                    if g == 0:
                        wait(pe, oT_ev, b.n)
                        pe.wait_ge(v_ev, 2 * b.n + 2)
                    for c in range(NCH):
                        n = CH if c < NCH - 1 else CM
                        for j in range(HG):
                            h = HG * g + j
                            mm = pe.matmul(ps[j * VC:(j + 1) * VC, B_O, g * L:(g + 1) * L], va[b.par][0:n, c, h, :],
                                           pr[0:n, h % (2 * HG), c * L:(c + 1) * L], start=(c == 0), stop=(c == NCH - 1))
                    mm.then_inc(pv_mm, 1)

                def turn_maximum(b, half):
                    pe.wait_ge(mxp_ok[half], b.n + 1)
                    bank = M1
                    if half == 0:
                        pe.wait_ge(v_ev, 2 * b.n + 1)
                    else:
                        bank = M2
                        wait(pe, lg_ev, b.n - 1)
                    pe.matmul(ps[0:SR + MR, bank, 0:L], mxp[:, half, :],
                              negid[:, :], start=True, stop=True).then_inc(mT_mm[half], 1)

                def keys(b, m):
                    if m == 0:
                        wait(pe, cx_in[b.par], 16 * b.half)
                        wait(pe, x2T_ev, b.n - 3)
                    else:
                        wait(pe, mT_ev[0], b.n - 1)
                    for k in range(KC):
                        mm = pe.matmul(ps[:, M0 + m, 0:CTX], wk_sb[:, k, m * P:(m + 1) * P], cx[b.par][:, k, :],
                                       start=(k == 0), stop=(k == KC - 1))
                    mm.then_inc(k_mm, 1)

                def queries(b):
                    pe.wait_ge(x1T_in, 16 * (b.n + 1))
                    wait(pe, mT_ev[1], b.n - 1)
                    for m in range(KC):
                        for k in range(KC):
                            mm = pe.matmul(ps[:, M2, m * L:(m + 1) * L], wq_sb[:, k, m * P:(m + 1) * P],
                                           x1T_sb[:, k, :], start=(k == 0), stop=(k == KC - 1))
                    mm.then_inc(q_mm, 1)

                def values(b, c):
                    bank, o = (M1, c * D) if c < 2 else (M2, 0)
                    for k in range(KC):
                        mm = pe.matmul(ps[0:CM, bank, o:o + D], cx[b.par][:, k, c * CH:c * CH + CM], wv_sb[:, k, :],
                                       start=(k == 0), stop=(k == KC - 1))
                    if c > 0:
                        mm.then_inc(v_mm, 1)

                def emit(b, kq, s, t, tail, more):
                    if kq and not t:
                        wait(pe, q_ev, b.n + 2)
                        keys(b + 2, 0)
                        keys(b + 2, 1)
                        queries(b + 2)
                    for h in range(H):
                        if s:
                            query_scores(b + 1, h)
                        if t:
                            key_scores(b, h)
                        if h == 0:
                            if tail:
                                weigh_values(b - 1, NG - 1)
                            if kq and t:
                                keys(b + 2, 0)
                        if h == 0 and t:
                            turn_maximum(b, 1)
                        if h == 1 and kq and t:
                            keys(b + 2, 1)
                        if h == 2 and kq and t:
                            queries(b + 2)
                        if h == 2 and tail:
                            pe.wait_ge(oT_ev, b.n)
                            if kq:
                                pe.wait_ge(k_ev, 2 * b.n + 5)
                            for g in range(NG):
                                mm = pe.transpose(ps[0:L, M0, g * P:(g + 1) * P], oT[:, g, :], ident[:, :])
                            mm.then_inc(o_mm, 1)
                        if h == 5 and tail:
                            pe.wait_ge(at_ok, b.n)
                            for k in range(KC):
                                mm = pe.transpose(ps[:, M0, k * L:(k + 1) * L], at[:, k * P:(k + 1) * P], ident[0:L, 0:L])
                            mm.then_inc(aT_mm, 1)
                        if h == 5 and s:
                            pe.wait_ge(k_ev, 2 * b.n + 6 if kq else 2 * NB)
                            if b.c >= 0:
                                wait(pe, mT_ev[0], b.n + 1)
                            values(b + 1, 0)
                        if h == 7 and s:
                            values(b + 1, 1)
                        if h == 9 and s:
                            if kq:
                                pe.wait_ge(q_ev, b.n + 3)
                            elif t:
                                pe.wait_ge(mT_ev[1], b.n + 1)
                            values(b + 1, 2)
                        if h == 6 and tail:
                            pe.wait_ge(aT_ev, b.n)
                            for k in range(KC):
                                mm = pe.matmul(ps[0:L, M0, 0:D], atT[:, k, :], wo_sb[:, k, :],
                                               start=(k == 0), stop=(k == KC - 1))
                            mm.then_inc(wo_mm, 1)
                        if h == 13 and tail:
                            pe.wait_ge(x2_ok, b.n)
                            for k in range(KC):
                                mm = pe.transpose(ps[:, M0, k * L:(k + 1) * L], x2[:, k * P:(k + 1) * P], ident[0:L, 0:L])
                            mm.then_inc(x2T_mm, 1)
                        if h == 11 and s:
                            turn_maximum(b + 1, 0)
                        if h == 15 and tail:
                            pe.wait_ge(x2T_ev, b.n)
                            if s:
                                pe.wait_ge(v_ev, 2 * b.n + 4)
                            elif t:
                                pe.wait_ge(mT_ev[1], b.n + 1)
                            for k in range(KC):
                                mm = pe.matmul(ps[0:L, M2, 0:E], x2T[:, k, :], ws_sb[:, k, :],
                                               start=(k == 0), stop=(k == KC - 1))
                            mm.then_inc(lg_mm, 1)
                        if t and h > 0 and h % HG == 0:
                            weigh_values(b, h // HG - 1)

                steps(emit, pe)

            @block.scalar
            def _(act):
                act.wait_ge(ones_set, 3)
                act.mul(bq4[:, :], bqk_sb[:, 0:KC], 1.0 / np.sqrt(DH)).then_inc(c_step, 1)
                act.wait_ge(c_ok, 1)

                def maximum_out(b, half):
                    act.wait_ge(mT_mm[half], b.n + 1)
                    bank = M1 if half == 0 else M2
                    act.activation(st[b.par][MS, half * HH:(half + 1) * HH, CTX:KQ],
                                   ps[MS, bank, 0:L].unsqueeze(1).to_broadcast([MR, HH, L]), ACT.Copy).then_inc(mT_ev[half], 1)

                def keys_out(b, m):
                    act.wait_ge(k_mm, 2 * b.n + m + 1)
                    wait(act, r_ok, 2 * b.n)
                    act.activation(kf[:, m, 0:CTX], ps[:, M0 + m, 0:CTX], ACT.Identity,
                                   bias=bqk_sb[:, KC + m:KC + m + 1]).then_inc(k_ev, 1)

                def emit(b, kq, s, t, tail, more):
                    for h in range(H):
                        if t:
                            act.wait_ge(t_mm, H * b.n + h + 1)
                            if h % HG == 0:
                                wait(act, pv_mm, NG * b.n + h // HG - 1)
                            act.activation(pr[:, h % (2 * HG), :], ps[0:CM, B_T + h % 2, 0:NCH * L], ACT.Exp).then_inc(exp_ok, 1)
                        if h == 0 and kq:
                            keys_out(b + 2, 0)
                        if h == 0 and tail:
                            act.wait_ge(pv_mm, NG * b.n)
                            act.activation(oT[:, :, :], ps[:, B_O, 0:NG * L].rearrange("p (g l) -> p g l", g=NG),
                                           ACT.Copy).then_inc(oT_ev, 1)
                        if h == 0 and t:
                            maximum_out(b, 1)
                        if h == 1 and kq:
                            keys_out(b + 2, 1)
                        if h == 2 and kq:
                            act.wait_ge(q_mm, b.n + 3)
                            for m in range(KC):
                                cp = act.activation(kf[:, m, CTX:KQ], ps[:, M2, m * L:(m + 1) * L], ACT.Identity,
                                                    bias=bq4[:, m:m + 1], scale=1.0 / np.sqrt(DH))
                            cp.then_inc(q_ev, 1)
                        if h == 5 and tail:
                            act.wait_ge(aT_mm, b.n)
                            act.activation(atT[:, :, :], ps[:, M0, 0:KC * L].rearrange("p (k l) -> p k l", k=KC),
                                           ACT.Copy).then_inc(aT_ev, 1)
                        if h in (4, 6) and kq:
                            m = (h - 4) // 2
                            pt = parts[b.par][:, m, :, :]
                            act.wait_ge(k1_ok, 2 * b.n + 5 + m)
                            act.activation(pt[:, 0:3:2, 0:CTX], pt[:, 4:5, 0:CTX].to_broadcast([P, 2, CTX]), ACT.Copy)
                            act.activation(pt[:, 3:6:2, CTX:KQ], pt[:, 4:5, CTX:KQ].to_broadcast([P, 2, L]), ACT.Copy)
                        if h in (5, 7) and kq:
                            m = (h - 5) // 2
                            pt = parts[b.par][:, m, :, :]
                            act.wait_ge(r_ok, 2 * b.n + 5 + m)
                            act.activation(pt[:, 1:4:2, 0:CTX], rf[:, m:m + 1, 0:CTX].to_broadcast([P, 2, CTX]), ACT.Copy)
                            act.activation(pt[:, 1:3, CTX:KQ], rf[:, m:m + 1, CTX:KQ].to_broadcast([P, 2, L]),
                                           ACT.Copy).then_inc(k2_ok, 1)
                        if h == 8 and s:
                            act.wait_ge(v_mm, 2 * b.n + 3)
                            wait(act, pv_mm, NG * b.n)
                            act.activation(va[(b + 1).par][:, 0:2, :, 0:DH],
                                           ps[0:CM, M1, :].rearrange("p (c h d) -> p c h d", c=2, h=H),
                                           ACT.Copy).then_inc(v_ev, 1)
                        if h == 10 and s:
                            act.wait_ge(v_mm, 2 * b.n + 4)
                            act.activation(va[(b + 1).par][:, 2, :, 0:DH],
                                           ps[0:CM, M2, 0:D].rearrange("p (h d) -> p h d", h=H),
                                           ACT.Copy).then_inc(v_ev, 1)
                        if h == 12 and s:
                            maximum_out(b + 1, 0)
                        if h == 13 and tail:
                            act.wait_ge(x2T_mm, b.n)
                            act.activation(x2T[:, :, :], ps[:, M0, 0:KC * L].rearrange("p (k l) -> p k l", k=KC),
                                           ACT.Copy).then_inc(x2T_ev, 1)
                        if h == 15 and tail:
                            act.wait_ge(lg_mm, b.n)
                            act.activation(LG[:, bass.ds(b.n - 1, 1), :], ps[0:L, M2, 0:E].unsqueeze(1),
                                           ACT.Copy).then_inc(lg_ev, 1)

                steps(emit, act)

            @block.vector
            def _(dve):
                dve.tensor_copy(bvr[:, :, :], bv_sb[:, :].unsqueeze(2).to_broadcast([P, KC, L])).then_inc(c_step, 1)
                dve.wait_ge(c_mm, 1)
                dve.tensor_tensor(cbc[:, :], ps[0:L, B_O, 0:D], bo_bc[:, :], ALU.add).then_inc(c_ok, 1)

                def first_part(b, m):
                    dve.wait_ge(k_ev, 2 * b.n + 2)
                    dve.wait_ge(q_ev, b.n + 1)
                    wait(dve, kq_in[m], 16 * SLOTS * (b.n - 1))
                    dve.tensor_copy(parts[b.par][:, m, 4, :], kf[:, m, :]).then_inc(k1_ok, 1)

                def rest(b, m):
                    dve.wait_ge(k1_ok, 2 * b.n + 1 + m)
                    dve.tensor_tensor(rf[:, m, :], kf[:, m, :], parts[b.par][:, m, 4, :], ALU.subtract).then_inc(r_ok, 1)

                def third_part(b, m):
                    dve.wait_ge(k2_ok, 2 * b.n + 1 + m)
                    for slot, one, c in ((5, 3, slice(0, CTX)), (0, 1, slice(CTX, KQ))):
                        k3 = dve.tensor_tensor(parts[b.par][:, m, slot, c], rf[:, m, c], parts[b.par][:, m, one, c],
                                               ALU.subtract)
                    k3.then_inc(k3_ok, 1)

                SPLIT_AT = {3: lambda b: first_part(b, 0), 4: lambda b: rest(b, 0), 5: lambda b: first_part(b, 1),
                            6: lambda b: rest(b, 1), 7: lambda b: third_part(b, 0), 12: lambda b: third_part(b, 1)}

                def emit(b, kq, s, t, tail, more):
                    if kq and not t:
                        for split in SPLIT_AT.values():
                            split(b + 2)
                    for h in range(H):
                        if s:
                            half, hh = divmod(h, HH)
                            dve.wait_ge(s_mm, H * b.n + H + h + 1)
                            if hh == 0:
                                wait(dve, mxp_ok[half], b.n + 1)
                            dve.tensor_reduce(mx[:, half, hh:hh + 1], ps[0:L, B_S + h % 2, 0:CTX], AX_X,
                                              ALU.max).then_inc(max_ok, 1)
                        if h == 2 and tail:
                            pv = ps[0:L, M0, :].rearrange("p (h w) -> p h w", h=H)
                            dve.wait_ge(o_mm, b.n)
                            dve.reciprocal(rc[:, :, :], pv[:, :, DH:VW]).then_inc(rc_ok, 1)
                            dve.wait_ge(rc_ok, b.n)
                            wait(dve, aT_mm, b.n - 1)
                            dve.tensor_tensor(at[:, :].rearrange("p (h d) -> p h d", h=H), pv[:, :, 0:DH],
                                              rc[:, :, :].to_broadcast([L, H, DH]), ALU.mult).then_inc(at_ok, 1)
                        if kq and t and h in SPLIT_AT:
                            SPLIT_AT[h](b + 2)
                        if h == 8 and tail:
                            dve.wait_ge(wo_mm, b.n)
                            dve.wait_ge(x1b_ok, b.n)
                            dve.tensor_tensor(xr[:, :], ps[0:L, M0, 0:D], x1b[:, :], ALU.add).then_inc(wo_rd, 1)
                        if h == 9 and tail:
                            dve.wait_ge(wo_rd, b.n)
                            dve.bn_stats(stats[:, :], xr[:, :]).then_inc(st_ok, 1)
                            dve.wait_ge(st_ok, b.n)
                            wait(dve, rstd_ok, b.n - 1)
                            stand(dve, dve_stands)
                            dve.bn_aggr(mv[:, :], stats[:, :]).then_inc(mv_ok, 1)
                        if h == 11 and tail:
                            dve.wait_ge(rstd_ok, b.n)
                            wait(dve, x2_out, 32 * (b.n - 1))
                            wait(dve, x2T_mm, b.n - 1)
                            dve.tensor_scalar(x2[:, :], xr[:, :], mv[:, 0:1], rstd[:, 0:1],
                                              ALU.subtract, ALU.mult).then_inc(x2_ok, 1)

                steps(emit, dve)


def experts(nc, ps, ident, LG, bs, wd, WG, WU, x2d, accd, out):
    with ExitStack() as ctx:
        def sb(name, shape, dt=F32):
            return ctx.enter_context(nc.sbuf_tensor(name, shape, dt))

        def sem(name):
            return ctx.enter_context(nc.semaphore(name))

        NBH = 2 * NB
        QN = NBH // 4
        JT = (T + P - 1) // P
        WD = sb("WD", [P, FC, E, D])
        bs_bc = sb("bs_bc", [L, E])
        lg = sb("lg", [L, NB, E])
        best = sb("best", [L, 2, NB])
        eq = sb("eq", [L, NB, E])
        top = sb("top", [L, NB])
        oh = sb("oh", [L, 2, NB, E])
        dm = sb("dm", [L, NB])
        e2 = sb("e2", [L, NB])
        den = sb("den", [L, NB])
        w = sb("w", [L, 2, NB])
        M = sb("M", [L, NB, E])
        pref = sb("pref", [L, E])
        before = sb("before", [L, L])
        ones = sb("ones", [L, L])
        run = [sb(f"run{u}", [L, NB // 2 + NB, E]) for u in range(2)]
        step = sb("step", [L, JT])
        more = sb("more", [L, E, JT])
        off = [sb(f"off{u}", [L, 2 * E]) for u in range(2)]
        off128 = sb("off128", [L, E])
        pos = sb("pos", [L, NB, E])
        posc = sb("posc", [L, 2, NB, E])
        place = sb("place", [L, 2, NB])
        place_i = sb("place_i", [L, 2, NB], I32)
        hi_i = sb("hi_i", [L, NBH], I32)
        lo_i = sb("lo_i", [L, NBH], I32)
        hi = sb("hi", [L, NBH])
        lo = sb("lo", [L, NBH])
        iot = sb("iot", [L, P])
        tok = sb("tok", [L, NB])
        ohl = sb("ohl", [L, NBH, P])
        ohh = sb("ohh", [L, NBH, TILES])
        rh = sb("rh", [L, NBH, 2, TILES])
        inv = sb("inv", [P, TILES])
        pad = sb("pad", [P, TILES])
        spare = sb("spare", [P, 1])
        spare_i = sb("spare_i", [P, 1], I32)
        gat = sb("gat", [P, TILES], I32)
        sca = sb("sca", [P, TILES], I32)
        wt = sb("wt", [P, TILES])
        tex = sb("tex", [L, TILES, E])
        texf = sb("texf", [L, TILES])
        expert_of = sb("expert_of", [L, TILES], I32)

        gi = sb("gi", [P, 2], U32)
        si = sb("si", [P, 2], U32)
        xs = sb("xs", [P, 2, D])
        xsT = sb("xsT", [P, 2, KC, P])
        sg = sb("sg", [P, 2, FH])
        hh = sb("hh", [P, 2, F])
        hT = sb("hT", [P, 2, FC, P])
        y = sb("y", [P, 2, D])

        acc = ohl[:, :, :].rearrange("p n c -> p (n c)").rearrange("p (b d) -> p b d", d=D)
        stats = sb("fstats", [L, NB, 6])
        mv = sb("fmv", [L, NB, 2])
        ve = sb("fve", [L, NB])
        rstd = sb("frstd", [L, NB])
        mhalf = sb("fmhalf", [L, NB])
        shift = sb("fshift", [L, NB])

        names = ("b_in wd_in set_a const chain dm_ok e2_ok M_ok cnt_mm rh_ok ohl_ok inv_mm lists_ok gi_ok si_ok xT_mm xT_ev "
                 "gu_mm sg_ok h_ok hT_mm hTa_ev hTb_ev y_mm y_ok added acc_in mv_ok ve_ok rstd_ok shift_ok res_ok st_ok out_sent").split()
        (b_in, wd_in, set_a, const, chain, dm_ok, e2_ok, M_ok, cnt_mm, rh_ok, ohl_ok, inv_mm, lists_ok, gi_ok, si_ok, xT_mm,
         xT_ev, gu_mm, sg_ok, h_ok, hT_mm, hTa_ev, hTb_ev, y_mm, y_ok, added, acc_in, mv_ok, ve_ok, rstd_ok, shift_ok, res_ok, st_ok,
         out_sent) = [sem("e_" + n) for n in names]
        pool_stands = sem("e_pool_stands")
        xs_in = [sem(f"xs_in{u}") for u in range(2)]
        acc_ins = [sem(f"acc_in{q}") for q in range(4)]

        B_G, B_U, B_H, B_Y, B_X = 0, 2, 4, 6, 7
        N_CONST = 11
        QB = NB // 4

        def steps(emit, eng):
            for t in range(-1, 3):
                emit(Step(0, t), t)
            with eng.Fori(0, (TILES - 6) // 2) as i:
                for c in (3, 4):
                    emit(Step(i, c), c)
            for t in range(TILES - 3, TILES + 1):
                emit(Step(0, t), t)

        with nc.Block() as block:

            @block.sync
            def _(sp):
                sp.dma_start(bs_bc[:, :], bs.partition_broadcast(L)).then_inc(b_in, 16)
                for c in range(FC - 1):
                    sp.dma_start(WD[:, c, :, :], wd[:, c * P:(c + 1) * P, :].rearrange("e p d -> p e d")).then_inc(wd_in, 16)
                sp.dma_start(WD[0:FR, FC - 1, :, :], wd[:, (FC - 1) * P:F, :].rearrange("e p d -> p e d"))\
                    .then_inc(wd_in, 16)
                sp.wait_ge(added, 16 * TILES)
                a = accd.rearrange("(b l) d -> l b d", l=L)
                for q in range(4):
                    sp.dma_start(acc[:, q * QB:(q + 1) * QB, :], a[:, q * QB:(q + 1) * QB, :]).then_inc(acc_ins[q], 16)
                for q in range(4):
                    sp.wait_ge(res_ok, q + 1)
                    sp.dma_start(out[q * QB:(q + 1) * QB, :, :].rearrange("b l d -> l b d"),
                                 acc[:, q * QB:(q + 1) * QB, :]).then_inc(out_sent, 16)
                sp.wait_ge(out_sent, 16 * 4)

            @block.gpsimd
            def _(pool):
                fl = dict(allow_small_or_imprecise_dtypes=True)
                pool.iota(pref[:, :], pattern=[[-1, E]], base=E, channel_multiplier=0, **fl).then_inc(const, 1)
                pool.memset(before[:, :], 1.0).then_inc(set_a, 1)
                pool.memset(ones[:, :], 1.0).then_inc(const, 1)
                for u in range(2):
                    pool.memset(run[u][:, 0:NB // 2, :], 0.0).then_inc(const, 1)
                    pool.memset(off[u][:, 0:E], 0.0).then_inc(const, 1)
                pool.iota(step[:, :], pattern=[[P, JT]], base=0, channel_multiplier=0, **fl).then_inc(const, 1)
                pool.iota(iot[:, :], pattern=[[1, P]], base=0, channel_multiplier=0, **fl).then_inc(const, 1)
                pool.iota(tok[:, :], pattern=[[L, NB]], base=1, channel_multiplier=1, **fl).then_inc(const, 1)
                pool.wait_ge(set_a, 1)
                pool.affine_select(out=before[:, :], in_=before[:, :], compare_op=ALU.is_gt, fill=0.0, base=0,
                                   pattern=[[1, L]], channel_multiplier=-1).then_inc(const, 1)
                pool.wait_ge(const, 10 - 1)
                pool.iota(spare[:, :], pattern=[[0, 1]], base=2 * T + 1, channel_multiplier=1, **fl).then_inc(const, 1)
                pool.wait_ge(const, 10)
                pool.memset(mhalf[:, :], -0.5).then_inc(const, 1)

                def gather(t):
                    wait(pool, xT_mm, t.n - 1)
                    stand(pool, pool_stands)
                    pool.tensor_copy(gi[:, t.par:t.par + 1].bitcast(I32), gat[:, bass.ds(t.n, 1)]).then_inc(gi_ok, 1)
                    pool.wait_ge(gi_ok, t.n + 1)
                    stand(pool, pool_stands)
                    pool.indirect_dma_start(xs[:, t.par, :], None, x2d,
                                            bass.IndirectOffsetOnAxis(ap=gi[:, t.par:t.par + 1], axis=0))\
                        .then_inc(xs_in[t.par], 16)

                def add_rows(t):
                    wait(pool, added, 16 * t.n)
                    stand(pool, pool_stands)
                    pool.tensor_copy(si[:, t.par:t.par + 1].bitcast(I32), sca[:, bass.ds(t.n, 1)]).then_inc(si_ok, 1)
                    pool.wait_ge(si_ok, t.n + 1)
                    pool.wait_ge(y_ok, t.n + 1)
                    stand(pool, pool_stands)
                    pool.indirect_dma_start(accd, bass.IndirectOffsetOnAxis(ap=si[:, t.par:t.par + 1], axis=0),
                                            y[:, t.par, :], None, compute_op=ALU.add, bounds_check=last_token,
                                            oob_is_err=False).then_inc(added, 16)

                pool.wait_ge(lists_ok, 3)
                last_token = pool.to_reg(T - 1)

                def emit(t, n):
                    if n == -1:
                        gather(t + 1)
                        gather(t + 2)
                    if n + 3 < TILES:
                        gather(t + 3)
                    if n - 1 >= 0:
                        add_rows(t - 1)

                steps(emit, pool)
                for q in range(4):
                    pool.wait_ge(mv_ok, q + 1)
                    s = slice(q * QB, (q + 1) * QB)
                    pool.tensor_scalar(ve[:, s], mv[:, s, 1], EPS, None, ALU.add).then_inc(ve_ok, 1)
                    pool.wait_ge(ve_ok, 2 * q + 1)
                    pool.tensor_tensor(rstd[:, s], ve[:, s], mhalf[:, s], ALU.pow).then_inc(rstd_ok, 1)
                    pool.wait_ge(rstd_ok, q + 1)
                    pool.tensor_tensor(shift[:, s], mv[:, s, 0], rstd[:, s], ALU.mult).then_inc(ve_ok, 1)
                    pool.wait_ge(ve_ok, 2 * q + 2)
                    pool.tensor_scalar_mul(shift[:, s], shift[:, s], -1.0).then_inc(shift_ok, 1)

            @block.tensor
            def _(pe):
                pe.wait_ge(const, N_CONST)
                pe.wait_ge(M_ok, 1)
                Mf = M[:, :, :].rearrange("p b e -> p (b e)")
                pe.matmul(ps[0:L, B_G, 0:NB * E], before[:, :], Mf, start=True, stop=True)
                pe.matmul(ps[0:L, B_G + 1, 0:NB * E], ones[:, :], Mf, start=True, stop=True).then_inc(cnt_mm, 1)
                pe.wait_ge(rh_ok, 1)
                for n in range(NBH):
                    if n % QN == 0:
                        pe.wait_ge(ohl_ok, n // QN + 1)
                    mm = pe.matmul(ps[:, B_Y, 0:2 * TILES], ohl[:, n, :], rh[:, n, :, :].rearrange("p a t -> p (a t)"),
                                   start=(n == 0), stop=(n == NBH - 1))
                mm.then_inc(inv_mm, 1)
                pe.wait_ge(lists_ok, 3)

                def turn_rows(t):
                    pe.wait_ge(xs_in[t.par], 16 * (t.half + 1))
                    wait(pe, xT_ev, t.n)
                    for k in range(KC):
                        mm = pe.transpose(ps[:, B_X, k * P:(k + 1) * P], xs[:, t.par, k * P:(k + 1) * P], ident[:, :])
                    mm.then_inc(xT_mm, 1)

                def expert(t):
                    return pe.value_load(expert_of[0:1, bass.ds(t.n, 1)], min_val=0, max_val=E - 1)

                def gate_up(t, e, halves):
                    pe.wait_ge(xT_ev, t.n + 1)
                    for f in halves:
                        wait(pe, h_ok, 2 * t.n + f - 1)
                        for bank, W in ((B_G, WG), (B_U, WU)):
                            for k in range(KC):
                                mm = pe.matmul(ps[:, bank + f, 0:FH], xsT[:, t.par, k, :],
                                               W[:, k, bass.ds(e, 1), f * FH:(f + 1) * FH],
                                               start=(k == 0), stop=(k == KC - 1))
                            mm.then_inc(gu_mm, 1)

                def turn_hidden(t):
                    pe.wait_ge(h_ok, 2 * t.n + 2)
                    wait(pe, hTa_ev, t.n)
                    wait(pe, hTb_ev, t.n)
                    for c in range(FC):
                        n = P if c < FC - 1 else FR
                        mm = pe.transpose(ps[0:n, B_H + c // 4, c % 4 * P:(c % 4 + 1) * P],
                                          hh[:, t.par, c * P:c * P + n], ident[:, :])
                        if c in (3, FC - 1):
                            mm.then_inc(hT_mm, 1)

                def down(t, e):
                    wait(pe, y_ok, t.n)
                    for c in range(FC):
                        n = P if c < FC - 1 else FR
                        if c == 0:
                            pe.wait_ge(hTa_ev, t.n + 1)
                        if c == 4:
                            pe.wait_ge(hTb_ev, t.n + 1)
                        mm = pe.matmul(ps[:, B_Y, 0:D], hT[0:n, t.par, c, :], WD[0:n, c, bass.ds(e, 1), :],
                                       start=(c == 0), stop=(c == FC - 1))
                    mm.then_inc(y_mm, 1)

                def emit(t, n):
                    if n == -1:
                        turn_rows(t + 1)
                    if n >= 1:
                        leaving = expert(t - 1)
                        turn_hidden(t - 1)
                    if n + 1 < TILES:
                        coming = expert(t + 1)
                        gate_up(t + 1, coming, (0,))
                    if n == 1:
                        pe.wait_ge(wd_in, 16 * FC)
                    if n >= 1:
                        down(t - 1, leaving)
                    if n + 2 < TILES:
                        turn_rows(t + 2)
                    if n + 1 < TILES:
                        gate_up(t + 1, coming, (1,))

                steps(emit, pe)

            @block.scalar
            def _(act):
                act.wait_ge(dm_ok, 1)
                act.activation(e2[:, :], dm[:, :], ACT.Exp).then_inc(e2_ok, 1)

                def rows_out(t):
                    act.wait_ge(xT_mm, t.n + 1)
                    wait(act, gu_mm, 4 * t.n - 4)
                    act.activation(xsT[:, t.par, :, :], ps[:, B_X, 0:KC * P].rearrange("p (k t) -> p k t", k=KC),
                                   ACT.Copy).then_inc(xT_ev, 1)

                def silus(t, halves):
                    for f in halves:
                        act.wait_ge(gu_mm, 4 * t.n + 2 * f + 1)
                        wait(act, h_ok, 2 * t.n + f - 1)
                        act.activation(sg[:, f, :], ps[:, B_G + f, 0:FH], ACT.Silu).then_inc(sg_ok, 1)

                def hidden_out(t):
                    act.wait_ge(hT_mm, 2 * t.n + 1)
                    act.activation(hT[:, t.par, 0:4, :], ps[:, B_H, :].rearrange("p (c t) -> p c t", c=4),
                                   ACT.Copy).then_inc(hTa_ev, 1)

                def emit(t, n):
                    if n == -1:
                        rows_out(t + 1)
                    if n >= 1:
                        hidden_out(t - 1)
                    if n + 1 < TILES:
                        silus(t + 1, (0,))
                    if n + 2 < TILES:
                        rows_out(t + 2)
                    if n + 1 < TILES:
                        silus(t + 1, (1,))

                steps(emit, act)
                for q in range(4):
                    act.wait_ge(shift_ok, q + 1)
                    for b in range(q * QB, (q + 1) * QB):
                        r = act.activation(acc[:, b, :], acc[:, b, :], ACT.Identity, bias=shift[:, b:b + 1],
                                           scale=rstd[:, b:b + 1])
                    r.then_inc(res_ok, 1)

            @block.vector
            def _(dve):
                done = [0]

                def link(ins):
                    done[0] += 1
                    ins.then_inc(chain, 1)
                    dve.wait_ge(chain, done[0])

                dve.wait_ge(b_in, 16)
                dve.wait_ge(const, N_CONST)
                bc = [L, NB, E]
                link(dve.tensor_tensor(lg[:, :, :], LG[:, :, :], bs_bc[:, :].unsqueeze(1).to_broadcast(bc), ALU.add))
                for s in range(2):
                    link(dve.tensor_reduce(best[:, s, :], lg[:, :, :], AX_X, ALU.max))
                    link(dve.tensor_tensor(eq[:, :, :], lg[:, :, :], best[:, s, :].unsqueeze(2).to_broadcast(bc),
                                           ALU.is_equal))
                    link(dve.tensor_tensor(eq[:, :, :], eq[:, :, :], pref[:, :].unsqueeze(1).to_broadcast(bc), ALU.mult))
                    link(dve.tensor_reduce(top[:, :], eq[:, :, :], AX_X, ALU.max))
                    link(dve.tensor_tensor(oh[:, s, :, :], eq[:, :, :], top[:, :].unsqueeze(2).to_broadcast(bc),
                                           ALU.is_equal))
                    if s == 0:
                        link(dve.scalar_tensor_tensor(out=lg[:, :, :], in0=oh[:, 0, :, :], scalar=-3e38, in1=lg[:, :, :],
                                                      op0=ALU.mult, op1=ALU.add))
                dve.tensor_tensor(M[:, :, :], oh[:, 0, :, :], oh[:, 1, :, :], ALU.add).then_inc(M_ok, 1)
                dve.tensor_tensor(dm[:, :], best[:, 1, :], best[:, 0, :], ALU.subtract).then_inc(dm_ok, 1)
                dve.wait_ge(e2_ok, 1)
                link(dve.tensor_scalar(den[:, :], e2[:, :], 1.0, None, ALU.add))
                link(dve.reciprocal(w[:, 0, :], den[:, :]))
                link(dve.tensor_tensor(w[:, 1, :], e2[:, :], w[:, 0, :], ALU.mult))
                dve.wait_ge(cnt_mm, 1)
                HB = NB // 2
                link(dve.tensor_copy(run[0][:, HB:, :], ps[0:L, B_G + 1, 0:NB * E].rearrange("p (b e) -> p b e", b=NB)))
                a = 0
                for sh in (1, 2, 4, 8):
                    link(dve.tensor_tensor(run[1 - a][:, HB:, :], run[a][:, HB:, :],
                                           run[a][:, HB - sh:HB + NB - sh, :], ALU.add))
                    a = 1 - a
                total = run[a][:, HB + NB - 1, :]
                link(dve.tensor_tensor(more[:, :, :], total.unsqueeze(2).to_broadcast([L, E, JT]),
                                       step[:, :].unsqueeze(1).to_broadcast([L, E, JT]), ALU.is_gt))
                link(dve.tensor_reduce(off[0][:, E:], more[:, :, :], AX_X, ALU.add))
                o = 0
                for sh in (1, 2, 4):
                    link(dve.tensor_tensor(off[1 - o][:, E:], off[o][:, E:], off[o][:, E - sh:2 * E - sh], ALU.add))
                    o = 1 - o
                first_tile = off[o][:, E - 1:2 * E - 1]
                link(dve.tensor_scalar(off128[:, :], first_tile, float(P), None, ALU.mult))
                link(dve.tensor_tensor(pos[:, :, :], ps[0:L, B_G, 0:NB * E].rearrange("p (b e) -> p b e", b=NB),
                                       run[a][:, HB - 1:HB + NB - 1, :], ALU.add))
                link(dve.tensor_tensor(pos[:, :, :], pos[:, :, :], off128[:, :].unsqueeze(1).to_broadcast(bc), ALU.add))
                for s in range(2):
                    pr = dve.tensor_tensor(posc[:, s, :, :], pos[:, :, :], oh[:, s, :, :], ALU.mult)
                link(pr)
                link(dve.tensor_reduce(place[:, :, :], posc[:, :, :, :], AX_X, ALU.add))
                link(dve.tensor_copy(place_i[:, :, :], place[:, :, :]))
                pf = place_i[:, :, :].rearrange("p s b -> p (s b)")
                dve.tensor_scalar(hi_i[:, :], pf, P.bit_length() - 1, None, ALU.logical_shift_right)
                link(dve.tensor_scalar(lo_i[:, :], pf, P - 1, None, ALU.bitwise_and))
                dve.tensor_copy(hi[:, :], hi_i[:, :])
                link(dve.tensor_copy(lo[:, :], lo_i[:, :]))
                link(dve.tensor_tensor(ohh[:, :, :], hi[:, :].unsqueeze(2).to_broadcast([L, NBH, TILES]),
                                       iot[:, 0:TILES].unsqueeze(1).to_broadcast([L, NBH, TILES]), ALU.is_equal))
                for s in range(2):
                    ss = slice(s * NB, (s + 1) * NB)
                    dve.tensor_tensor(rh[:, ss, 0, :], ohh[:, ss, :],
                                      tok[:, :].unsqueeze(2).to_broadcast([L, NB, TILES]), ALU.mult)
                    r = dve.tensor_tensor(rh[:, ss, 1, :], ohh[:, ss, :],
                                          w[:, s, :].unsqueeze(2).to_broadcast([L, NB, TILES]), ALU.mult)
                r.then_inc(rh_ok, 1)
                for n in range(0, NBH, QN):
                    dve.tensor_tensor(ohl[:, n:n + QN, :], lo[:, n:n + QN].unsqueeze(2).to_broadcast([L, QN, P]),
                                      iot[:, :].unsqueeze(1).to_broadcast([L, QN, P]), ALU.is_equal).then_inc(ohl_ok, 1)
                link(dve.tensor_tensor(tex[:, :, :], iot[:, 0:TILES].unsqueeze(2).to_broadcast([L, TILES, E]),
                                       first_tile.unsqueeze(1).to_broadcast([L, TILES, E]), ALU.is_ge))
                link(dve.tensor_reduce(texf[:, :], tex[:, :, :], AX_X, ALU.add))
                dve.tensor_scalar(expert_of[:, :], texf[:, :], -1.0, None, ALU.add).then_inc(lists_ok, 1)
                dve.wait_ge(inv_mm, 1)
                dve.tensor_copy(wt[:, :], ps[:, B_Y, TILES:2 * TILES]).then_inc(chain, 1)
                done[0] += 1
                link(dve.tensor_copy(inv[:, :], ps[:, B_Y, 0:TILES]))
                dve.tensor_scalar(gat[:, :], inv[:, :], -1.0, 0.0, ALU.add, ALU.max).then_inc(lists_ok, 1)
                link(dve.tensor_scalar(pad[:, :], inv[:, :], 0.0, spare[:, 0:1], ALU.is_equal, ALU.mult))
                dve.scalar_tensor_tensor(out=sca[:, :], in0=inv[:, :], scalar=-1.0, in1=pad[:, :], op0=ALU.add,
                                         op1=ALU.add).then_inc(lists_ok, 1)

                def hidden(t, halves):
                    for f in halves:
                        dve.wait_ge(sg_ok, 2 * t.n + f + 1)
                        dve.wait_ge(gu_mm, 4 * t.n + 2 * f + 2)
                        wait(dve, hT_mm, 2 * t.n - 2)
                        dve.tensor_tensor(hh[:, t.par, f * FH:(f + 1) * FH], sg[:, f, :], ps[:, B_U + f, 0:FH],
                                          ALU.mult).then_inc(h_ok, 1)

                def hidden_out(t):
                    dve.wait_ge(hT_mm, 2 * t.n + 2)
                    dve.tensor_copy(hT[:, t.par, 4, :], ps[:, B_H + 1, 0:P])
                    dve.tensor_copy(hT[0:FR, t.par, 5, :], ps[0:FR, B_H + 1, P:2 * P]).then_inc(hTb_ev, 1)

                def weigh(t):
                    dve.wait_ge(y_mm, t.n + 1)
                    wait(dve, added, 16 * (t.n - 1))
                    dve.tensor_scalar(y[:, t.par, :], ps[:, B_Y, 0:D], wt[:, bass.ds(t.n, 1)], None,
                                      ALU.mult).then_inc(y_ok, 1)

                def emit(t, n):
                    if n >= 1:
                        hidden_out(t - 1)
                    if n + 1 < TILES:
                        hidden(t + 1, (0,))
                    if n >= 1:
                        weigh(t - 1)
                    if n + 1 < TILES:
                        hidden(t + 1, (1,))

                steps(emit, dve)

                def last_stats(q):
                    dve.wait_ge(acc_ins[q], 16)
                    for b in range(q * QB, (q + 1) * QB):
                        s = dve.bn_stats(stats[:, b, :], acc[:, b, :])
                    s.then_inc(st_ok, 1)
                    dve.wait_ge(st_ok, q + 1)
                    for b in range(q * QB, (q + 1) * QB):
                        m = dve.bn_aggr(mv[:, b, :], stats[:, b, :])
                    m.then_inc(mv_ok, 1)

                for q in range(4):
                    last_stats(q)


def decoder_layer(nc, x, xT, ctxT, sa_wqT, sa_wqkvT, sa_bqk, sa_bqkv, sa_wop, sa_w2T, sa_b2, wqT, wkT, wvT, woT, bqk, bv,
                  bo, ws, bs, wg, wu, wd, out):
    x1d = nc.dram_tensor("x1d", (NB, L, D), F32, kind="Internal").ap()
    x1Td = nc.dram_tensor("x1Td", (NB, P, KC, L), F32, kind="Internal").ap()
    x2d = nc.dram_tensor("x2d", (T, D), F32, kind="Internal").ap()
    accd = nc.dram_tensor("accd", (T, D), F32, kind="Internal").ap()
    with ExitStack() as ctx:
        ps = ctx.enter_context(nc.psum_tensor("ps", [P, 8, 512], F32))
        ident = ctx.enter_context(nc.sbuf_tensor("ident", [P, P], F32))
        LG = ctx.enter_context(nc.sbuf_tensor("LG", [L, NB, E], F32))
        WG = ctx.enter_context(nc.sbuf_tensor("WG", [P, KC, E, F], F32))
        WU = ctx.enter_context(nc.sbuf_tensor("WU", [P, KC, E, F], F32))
        with ExitStack() as until_experts:
            cross = CrossOperands(nc, until_experts, ctxT, wqT, wkT, wvT, woT, bqk, bv, bo, ws)
            self_attention(nc, ps, ident, x, xT, sa_wqT, sa_wqkvT, sa_bqk, sa_bqkv, sa_wop, sa_w2T, sa_b2, wg, wu, WG, WU,
                           cross, x1d, x1Td)
            cross_attention(nc, ps, ident, ctxT, cross, x1d, x1Td, x2d, accd, LG)
        experts(nc, ps, ident, LG, bs, wd, WG, WU, x2d, accd, out)


def kernel(**inputs):
    import concourse.bacc as bacc
    from concourse.bass_utils import run_bass_kernel_spmd

    a = {k: np.asarray(v) for k, v in inputs.items()}

    def chunked(w):
        return w.reshape(-1, P, w.shape[-1]).transpose(1, 0, 2)

    def columns(v):
        return v.reshape(-1, P).T

    turned = np.arange(D).reshape(KC, P // DH, DH).transpose(0, 2, 1).reshape(-1)
    sa, xa = "L0_attn_", "L0_xattn_"
    lay = {
        "x": a["x"],
        "xT": chunked(a["x"].reshape(T, D).T),
        "ctxT": a["ctx_1024"].transpose(0, 2, 1).reshape(NB, KC, P, CTX).transpose(0, 2, 1, 3),
        "sa_wqT": chunked(a[sa + "Wq"].T),
        "sa_wqkvT": chunked(a[sa + "Wqkv"].T),
        "sa_bqk": columns(a[sa + "bqkv"][0:2 * D]),
        "sa_bqkv": a[sa + "bqkv"],
        "sa_wop": a[sa + "Wop"],
        "sa_w2T": a[sa + "W2"].T,
        "sa_b2": a[sa + "b2"],
        "wqT": chunked(a[xa + "wq"][turned].T),
        "wkT": chunked(a[xa + "wk"][turned].T),
        "wvT": chunked(a[xa + "wv"].T),
        "woT": chunked(a[xa + "wo"].T),
        "bqk": columns(np.concatenate([a[xa + "bq"][turned], a[xa + "bk"][turned]])),
        "bv": columns(a[xa + "bv"]),
        "bo": a[xa + "bo"],
        "ws": chunked(a["L0_ffn_Ws"]),
        "bs": a["L0_ffn_bs"],
        "wg": a["L0_ffn_Wg"],
        "wu": a["L0_ffn_Wu"],
        "wd": a["L0_ffn_Wd"],
    }
    nc = bacc.Bacc("TRN2", target_bir_lowering=False, num_devices=1)
    arrays, args = {}, {}
    for name, v in lay.items():
        v = np.ascontiguousarray(v)
        arrays["in_" + name] = v
        args[name] = nc.dram_tensor("in_" + name, v.shape, mybir.dt.from_np(v.dtype), kind="ExternalInput").ap()
    out = nc.dram_tensor("out", (NB, L, D), F32, kind="ExternalOutput").ap()
    decoder_layer(nc, **args, out=out)
    r = run_bass_kernel_spmd(nc, [arrays], core_ids=[0])
    return r.results[0]["out"]
```
